# Optimizing a Trainium2 kernel written in Bass

```python
import numpy as np
import jax
import jax.numpy as jnp

def _softmax(x, axis=-1):
    return jax.nn.softmax(x, axis=axis)

def _gelu(x):
    return jax.nn.gelu(x, approximate=True)

def _silu(x):
    return jax.nn.silu(x)

def _sigmoid(x):
    return jax.nn.sigmoid(x)

def _layernorm(x, axis=-1, eps=1e-05):
    m = jnp.mean(x, axis=axis, keepdims=True)
    v = jnp.var(x, axis=axis, keepdims=True)
    return (x - m) / jnp.sqrt(v + eps)

def _scatter_add(tgt, idx, src, axis=0):
    return tgt.at[idx].add(src)

def _segment_sum(src, seg, n):
    return jax.ops.segment_sum(src, seg, n)
kernel_name = 'mk_gnn_resnorm_d4_gnn_r8_ed35a4'

def setup_inputs(seed: int=0):
    np.random.seed(seed)
    _w = jnp.asarray

    def _rec_inputs():
        import jax
        import jax.numpy as jnp
        _gk = jax.random.key(seed)
        x = -0.0005121 + 1.001 * jax.random.normal(jax.random.fold_in(_gk, 1), (12500, 64), jnp.float32)
        _s = jax.random.randint(jax.random.fold_in(_gk, 2), (100000,), 0, 12500, jnp.int32)
        _d = jax.random.randint(jax.random.fold_in(_gk, 3), (100000,), 0, 12500, jnp.int32)
        _loop = jnp.arange(12500, dtype=jnp.int32)
        src = jnp.concatenate([_s, _d, _loop])
        dst = jnp.concatenate([_d, _s, _loop])
        _o = jnp.argsort(dst, stable=True)
        src = src[_o]
        dst = dst[_o]
        edge_attr_5 = jax.random.uniform(jax.random.fold_in(_gk, 12), (212500, 5), jnp.float32, 0.0, 1)
        edge_type_16 = jax.random.randint(jax.random.fold_in(_gk, 14), (212500,), 0, 16, jnp.int32)
        edge_weight = jax.random.uniform(jax.random.fold_in(_gk, 15), (212500,), jnp.float32, 0.0, 1)
        return (x, src, dst, edge_attr_5, edge_type_16, edge_weight)
    x, src, dst, edge_attr_5, edge_type_16, edge_weight = _rec_inputs()

    def _L0_gnn_setup():
        import jax, jax.numpy as jnp
        import numpy as np
        EMB = 64
        HEADS = 2
        NUM_BOND = 5
        NEG_SLOPE = 0.2
        key = jax.random.key(seed)
        ks = jax.random.split(key, 9)
        N, E = (6250, 100000)
        x = jax.random.normal(ks[0], (N, EMB), dtype=jnp.float32)
        edge_index = jax.random.randint(ks[1], (2, E), 0, N, dtype=jnp.int64)
        edge_attr = jax.random.uniform(ks[2], (E, NUM_BOND), dtype=jnp.float32)
        W_lin = jax.random.normal(ks[3], (EMB, HEADS * EMB), dtype=jnp.float32) / np.sqrt(EMB)
        b_lin = jnp.zeros((HEADS * EMB,), dtype=jnp.float32)
        W_edge = jax.random.normal(ks[4], (NUM_BOND, HEADS * EMB), dtype=jnp.float32) / np.sqrt(NUM_BOND)
        b_edge = jnp.zeros((HEADS * EMB,), dtype=jnp.float32)
        att = jax.random.normal(ks[5], (1, HEADS, 2 * EMB), dtype=jnp.float32) / np.sqrt(2 * EMB)
        bias = jnp.zeros((EMB,), dtype=jnp.float32)
        return {'x': x, 'edge_index': edge_index, 'edge_attr': edge_attr, 'W_lin': W_lin, 'b_lin': b_lin, 'W_edge': W_edge, 'b_edge': b_edge, 'att': att, 'bias': bias}
    _L0_gnn_all = _L0_gnn_setup()
    _L0_gnn_in = {k: v for k, v in _L0_gnn_all.items() if k in ('W_lin', 'b_lin', 'W_edge', 'b_edge', 'att', 'bias')}
    del _L0_gnn_all

    def _L1_gnn_setup():
        import jax, jax.numpy as jnp
        import numpy as np
        N_NODES = 6250
        N_EDGES = 100000
        D_IN = 64
        D_OUT = 64
        NUM_RELS = 16
        key = jax.random.key(seed)
        k1, k2, k3, k4, k5 = jax.random.split(key, 5)
        feat = jax.random.normal(k1, (N_NODES, D_IN), dtype=jnp.float32)
        weight = jax.random.normal(k2, (NUM_RELS, D_IN, D_OUT), dtype=jnp.float32) * 0.05
        src = jax.random.randint(k3, (N_EDGES,), 0, N_NODES, dtype=jnp.int32)
        dst = jax.random.randint(k4, (N_EDGES,), 0, N_NODES, dtype=jnp.int32)
        etypes = jax.random.randint(k5, (N_EDGES,), 0, NUM_RELS, dtype=jnp.int32)
        return {'feat': feat, 'weight': weight, 'src': src, 'dst': dst, 'etypes': etypes}
    _L1_gnn_all = _L1_gnn_setup()
    _L1_gnn_in = {k: v for k, v in _L1_gnn_all.items() if k in ('weight',)}
    del _L1_gnn_all

    def _L2_gnn_setup():
        import jax, jax.numpy as jnp
        import numpy as np
        N, F, E = (6250, 64, 156250)
        key = jax.random.key(seed)
        k1, k2, k3 = jax.random.split(key, 3)
        x = jax.random.normal(k1, (N, F), dtype=jnp.float32)
        edge_weight = jax.random.uniform(k2, (E,), dtype=jnp.float32)
        edge_index = jax.random.randint(k3, (2, E), 0, N, dtype=jnp.int64)
        return {'x': x, 'edge_weight': edge_weight, 'edge_index': edge_index}
    _L2_gnn_all = _L2_gnn_setup()
    _L2_gnn_in = {k: v for k, v in _L2_gnn_all.items() if k in ()}
    del _L2_gnn_all

    def _L3_gnn_setup():
        import jax, jax.numpy as jnp
        import numpy as np
        N_NODES = 12500
        N_EDGES = 200000
        D_IN = 64
        D_OUT = 64
        key = jax.random.key(seed)
        k1, k2, k3, k4 = jax.random.split(key, 4)
        feat = jax.random.normal(k1, (N_NODES, D_IN), dtype=jnp.float32)
        edge_src = jax.random.randint(k2, (N_EDGES,), 0, N_NODES, dtype=jnp.int64)
        edge_dst = jax.random.randint(k3, (N_EDGES,), 0, N_NODES, dtype=jnp.int64)
        gain = float(np.sqrt(2.0))
        limit = gain * float(np.sqrt(6.0 / (D_IN + D_OUT)))
        fc_weight = jax.random.uniform(k4, (D_OUT, D_IN), dtype=jnp.float32, minval=-limit, maxval=limit)
        return {'feat': feat, 'edge_src': edge_src, 'edge_dst': edge_dst, 'fc_weight': fc_weight}
    _L3_gnn_all = _L3_gnn_setup()
    _L3_gnn_in = {k: v for k, v in _L3_gnn_all.items() if k in ('fc_weight',)}
    del _L3_gnn_all
    return {'x': x, 'src': src, 'dst': dst, 'edge_attr_5': edge_attr_5, 'edge_type_16': edge_type_16, 'edge_weight': edge_weight, 'L0_gnn_W_lin': _L0_gnn_in['W_lin'], 'L0_gnn_b_lin': _L0_gnn_in['b_lin'], 'L0_gnn_W_edge': _L0_gnn_in['W_edge'], 'L0_gnn_b_edge': _L0_gnn_in['b_edge'], 'L0_gnn_att': _L0_gnn_in['att'], 'L0_gnn_bias': _L0_gnn_in['bias'], 'L1_gnn_weight': _L1_gnn_in['weight'], 'L3_gnn_fc_weight': _L3_gnn_in['fc_weight']}

def reference(x, src, dst, edge_attr_5, edge_type_16, edge_weight, L0_gnn_W_lin, L0_gnn_b_lin, L0_gnn_W_edge, L0_gnn_b_edge, L0_gnn_att, L0_gnn_bias, L1_gnn_weight, L3_gnn_fc_weight):
    import jax
    import jax.numpy as jnp

    def _L0_gnn_ref(x, edge_index, edge_attr, W_lin, b_lin, W_edge, b_edge, att, bias):
        import jax, jax.numpy as jnp
        import numpy as np
        EMB = 64
        HEADS = 2
        NUM_BOND = 5
        NEG_SLOPE = 0.2
        N = x.shape[0]
        h = (x @ W_lin + b_lin).reshape(N, HEADS, EMB)
        ee = (edge_attr @ W_edge + b_edge).reshape(-1, HEADS, EMB)
        src = edge_index[0]
        dst = edge_index[1]
        x_i = h[src]
        x_j = h[dst] + ee
        att_i, att_j = (att[..., :EMB], att[..., EMB:])
        alpha = (x_i * att_i).sum(-1) + (x_j * att_j).sum(-1)
        alpha = jnp.where(alpha >= 0, alpha, NEG_SLOPE * alpha)
        amax = jax.ops.segment_max(alpha, src, num_segments=N)
        e = jnp.exp(alpha - amax[src])
        denom = jax.ops.segment_sum(e, src, num_segments=N)
        alpha = e / (denom[src] + 1e-16)
        messages = x_j * alpha[:, :, None]
        out = jax.ops.segment_sum(messages, src, num_segments=N)
        out = out.mean(axis=1) + bias
        return out

    def _L1_gnn_ref(feat, weight, src, dst, etypes):
        import jax, jax.numpy as jnp
        import numpy as np
        N_NODES = 6250
        N_EDGES = 100000
        D_IN = 64
        D_OUT = 64
        NUM_RELS = 16
        num_rels = weight.shape[0]
        h_src = feat[src]
        msg = jnp.zeros((h_src.shape[0], weight.shape[2]), dtype=feat.dtype)
        for r in range(num_rels):
            mask = etypes == r
            msg = msg + h_src * mask[:, None].astype(feat.dtype) @ weight[r]
        out = jax.ops.segment_sum(msg, dst, num_segments=feat.shape[0])
        return out

    def _L2_gnn_ref(x, edge_weight, edge_index):
        import jax, jax.numpy as jnp
        import numpy as np
        N, F, E = (6250, 64, 156250)
        src = edge_index[0]
        dst = edge_index[1]
        msg = x[src] * edge_weight[:, None]
        out = jax.ops.segment_sum(msg, dst, num_segments=x.shape[0])
        return out

    def _L3_gnn_ref(feat, edge_src, edge_dst, fc_weight):
        import jax, jax.numpy as jnp
        import numpy as np
        N_NODES = 12500
        N_EDGES = 200000
        D_IN = 64
        D_OUT = 64
        h_src = feat[edge_src]
        h_dst = feat[edge_dst]
        a = jnp.sum(h_src * h_dst, axis=-1, keepdims=True)
        m = h_src * a
        neigh = jax.ops.segment_sum(m, edge_dst, num_segments=feat.shape[0])
        return neigh @ fc_weight.T
    edge_index = jnp.stack([src, dst])
    x = _layernorm(x + _L0_gnn_ref(x, edge_index, edge_attr_5, L0_gnn_W_lin, L0_gnn_b_lin, L0_gnn_W_edge, L0_gnn_b_edge, L0_gnn_att, L0_gnn_bias), axis=-1)
    x = _layernorm(x + _L1_gnn_ref(x, L1_gnn_weight, src, dst, edge_type_16), axis=-1)
    x = _layernorm(x + _L2_gnn_ref(x, edge_weight, edge_index), axis=-1)
    x = _layernorm(x + _L3_gnn_ref(x, src, dst, L3_gnn_fc_weight), axis=-1)
    return x

_drawn_inputs = setup_inputs


def setup_inputs(seed=0):
    import zlib

    import numpy as np

    out = dict(_drawn_inputs(seed))
    spreads = {'L0_gnn_b_lin': (0.0, 0.1), 'L0_gnn_b_edge': (0.0, 0.1), 'L0_gnn_bias': (0.0, 0.1)}
    factors = {}
    for name, (base, spread) in spreads.items():
        noise = np.random.default_rng([zlib.crc32(name.encode()), seed]).standard_normal(out[name].shape)
        drawn = base * np.exp(spread * noise) if base else spread * noise
        out[name] = jnp.asarray(drawn.astype(out[name].dtype))
    for name, factor in factors.items():
        out[name] = (out[name] * factor).astype(out[name].dtype)
    return out
```

```python
from contextlib import ExitStack

import concourse.bass as bass
from concourse import mybir

P = 128
N = 12500
E = 212500
D = 64
HEADS = 2
BOND = 5
RELS = 16
NEG_SLOPE = 0.2
EPS = 1e-5
U = 8
NB = -(-N // P)
NP = NB * P
NT = -(-E // (P * U)) * U
EP = NT * P
LASTC = E - (P - 1) * NT
FULLN = N // P
RESTN = N - FULLN * P
PADNODE = NP - 1
VISITS = NT + NB - 1
NV = -(-VISITS // U) * U
GT = NT // P
GV = -(-NV // P)
NVP = GV * P
assert NT % P == 0 and PADNODE >= N and 0 < LASTC < NT

C_Z = D
C_KEY = C_Z + HEADS
C_ATTR = C_KEY + 1
C_ONE = C_ATTR + BOND
ROW = C_ONE + 1
ROWP = 76
LOW = -3.0e38

F32 = mybir.dt.float32
BF16 = mybir.dt.bfloat16
I32 = mybir.dt.int32
ALU = mybir.AluOpType
ACT = mybir.ActivationFunctionType
X_AXIS = mybir.AxisListType.X


class Chain:

    def __init__(self, eng, sem):
        self.eng, self.sem, self.n = eng, sem, 0

    def add(self, ins):
        self.n += 1
        return ins.then_inc(self.sem, 1)

    def link(self, ins):
        self.add(ins)
        self.eng.wait_ge(self.sem, self.n)


class Stage:

    def __init__(self, nc, name):
        self.nc, self.name, self.ctx, self.sems = nc, name, ExitStack(), []

    whole = None

    def __enter__(self):
        return self

    def __exit__(self, *a):
        for sem in self.sems:
            self.nc.gpsimd.sem_clear(sem)
        return self.ctx.__exit__(*a)

    def sb(self, name, shape, dt=F32):
        return self.ctx.enter_context(self.nc.sbuf_tensor(f"{self.name}_{name}", shape, dt))

    def ps(self, name, shape, dt=F32):
        return self.ctx.enter_context(self.nc.psum_tensor(f"{self.name}_{name}", shape, dt))

    def sem(self, name):
        self.sems.append(self.ctx.enter_context(self.nc.semaphore(f"{self.name}_{name}")))
        return self.sems[-1]

    def pool_dma_sem(self, name):
        return Stage.whole.enter_context(self.nc.semaphore(f"{self.name}_{name}"))


def wait_apart(eng, passed, sem, value):
    eng.wait_ge(sem, value)
    eng.sem_inc(passed, 1)


def at(c):
    return bass.ds(c, 1)


def load_registers(nc, engine, row, i, high, why):
    _, values = nc.values_load_multi_w_load_instructions(
        row[0:1, bass.ds(i * U, U)], engines=[engine], min_val=0, max_val=high,
        skip_runtime_bounds_check_because=why)
    return values


def constants(nc, K):
    with Stage(nc, "const") as s:
        ints = s.sb("ints", [P, P + 1], I32)
        made, chain = s.sem("made"), s.sem("chain")
        with nc.Block() as block:
            @block.gpsimd
            def _(pool):
                pool.iota(ints[:, 0:P], [[1, P]], base=0, channel_multiplier=0)
                pool.iota(ints[:, P:P + 1], [[0, 1]], base=0, channel_multiplier=1)
                pool.iota(K.visit_i[:, :], [[P, GV]], base=0, channel_multiplier=1)
                pool.iota(K.edges_i[:, :], [[P, NB]], base=P, channel_multiplier=0).then_inc(made, 1)

            @block.vector
            def _(v):
                c = Chain(v, chain)
                v.wait_ge(made, 1)
                v.memset(K.ones[:, :], 1.0)
                v.tensor_copy(K.visit[:, :], K.visit_i[:, :])
                v.tensor_copy(K.edges[:, :], K.edges_i[:, :])
                v.tensor_copy(K.pcol[:, :], ints[:, P:P + 1])
                c.link(v.tensor_copy(K.iota[:, :], ints[:, 0:P]))
                v.tensor_copy(K.iota_b[:, :], K.iota[:, :])
                v.tensor_scalar(K.below[:, :], K.iota[:, :], K.pcol[:, 0:1], None, ALU.is_lt)
                v.tensor_scalar(K.above[:, :], K.iota[:, :], K.pcol[:, 0:1], None, ALU.is_gt)
                c.link(v.tensor_scalar(K.ident[:, :], K.iota[:, :], K.pcol[:, 0:1], None, ALU.is_equal))
                v.tensor_copy(K.ident_b[:, :], K.ident[:, :])
                v.tensor_scalar(K.ident_128[:, :], K.ident[:, :], float(P), None, ALU.mult)


def load_edges(nc, K, A, src, dst, etype, weight, x, M):
    with Stage(nc, "edges") as s:
        typ = s.sb("typ", [P, NT], I32)
        w = s.sb("w", [P, NT])
        a1 = s.sb("a1", [P, NT])
        d1 = s.sb("d1", [P, NT])
        padded, loaded, ready, stored, chain = s.sem("padded"), s.sem("loaded"), s.sem("ready"), s.sem("stored"), s.sem("chain")
        with nc.Block() as block:
            @block.sync
            def _(sp):
                sp.wait_ge(padded, 1)
                for where, what in ((A.src_i, src), (A.dst_i, dst), (typ, etype), (w, weight)):
                    sp.dma_start(where[0:P - 1, 0:NT], what[0:(P - 1) * NT].rearrange("(p c) -> p c", c=NT)).then_inc(loaded, 16)
                    sp.dma_start(where[P - 1:P, 0:LASTC], what[(P - 1) * NT:E].rearrange("(p c) -> p c", p=1)).then_inc(loaded, 16)
                sp.dma_start(K.x[:, 0:FULLN, :], x[0:FULLN * P, :].rearrange("(b p) d -> p b d", p=P)).then_inc(loaded, 16)
                sp.dma_start(K.x[0:RESTN, FULLN, :], x[FULLN * P:N, :]).then_inc(loaded, 16)
                sp.wait_ge(ready, 1)
                sp.dma_start(M.src.rearrange("(p c) -> p c", c=NT), A.src_f[:, :]).then_inc(stored, 16)
                sp.dma_start(M.dst.rearrange("(p c) -> p c", c=NT), d1[:, :]).then_inc(stored, 16)
                sp.dma_start(M.relrow.rearrange("(p c) -> p c", c=NT), a1[:, :]).then_inc(stored, 16)
                sp.dma_start(M.weight.rearrange("(p c) -> p c", c=NT), w[:, :]).then_inc(stored, 16)
                sp.wait_ge(stored, 64)

            @block.vector
            def _(v):
                c = Chain(v, chain)
                v.memset(A.src_i[:, :], PADNODE)
                v.memset(A.dst_i[:, :], PADNODE)
                v.memset(typ[:, :], 0)
                v.memset(w[:, :], 0.0)
                c.link(v.memset(K.x[:, :, :], 0.0))
                v.sem_inc(padded, 1)
                v.wait_ge(loaded, 160)
                v.tensor_copy(A.src_f[:, :], A.src_i[:, :])
                v.tensor_copy(d1[:, :], A.dst_i[:, 0:NT])
                c.link(v.tensor_copy(a1[:, :], typ[:, :]))
                v.scalar_tensor_tensor(a1[:, :], A.src_f[:, :], float(RELS), a1[:, :], ALU.mult, ALU.add).then_inc(ready, 1)


def split_keys(nc, A, s):
    tmp_lo, tmp_hi, chain = s.sb("tmp_lo", [P, NT], I32), s.sb("tmp_hi", [P, NT], I32), s.sem("split_chain")
    with nc.Block() as block:
        @block.vector
        def _(v):
            c = Chain(v, chain)
            v.tensor_scalar(tmp_lo[:, :], A.key_i[:, :], P - 1, None, ALU.bitwise_and)
            c.link(v.tensor_scalar(tmp_hi[:, :], A.key_i[:, :], 7, None, ALU.logical_shift_right))
            v.tensor_copy(A.lo_f[:, :], tmp_lo[:, :])
            v.tensor_copy(A.hi_f[:, :], tmp_hi[:, :])
            v.tensor_copy(A.lo[:, :], tmp_lo[:, :])
            c.link(v.tensor_copy(A.hi[:, :], tmp_hi[:, :]))


def count_places(nc, K, A, name):
    with Stage(nc, name) as s:
        onehot_lo = s.sb("onehot_lo", [P, U, P], BF16)
        onehot_hi = s.sb("onehot_hi", [P, U, NB], BF16)
        counts = s.sb("counts", [P, NB])
        totals = s.sb("totals", [P, NB])
        upto = s.sb("upto", [P, NB])
        zeros = s.sb("zeros", [P, NB])
        zeros_b = s.sb("zeros_b", [P, P], BF16)
        ps_count = s.ps("ps_count", [P, 512])
        ps_sums = s.ps("ps_sums", [P, 512])
        chain, hot, used, copied, summed = [s.sem(n) for n in ("chain", "hot", "used", "copied", "summed")]
        with nc.Block() as block:
            @block.vector
            def _(v):
                c = Chain(v, chain)
                v.memset(zeros[:, :], 0.0)
                v.memset(zeros_b[:, :], 0.0).then_inc(hot, 1)
                with v.Fori(0, NT // U) as i:
                    v.wait_ge(used, i + 1)
                    for k in range(U):
                        v.tensor_scalar(onehot_lo[:, k, :], K.iota_b[:, :], A.lo_f[:, at(i * U + k)], None, ALU.is_equal)
                        v.tensor_scalar(onehot_hi[:, k, :], K.iota_b[:, 0:NB], A.hi_f[:, at(i * U + k)], None,
                                        ALU.is_equal).then_inc(hot, 1)
                v.wait_ge(used, NT // U + 1)
                v.tensor_copy(counts[:, :], ps_count[:, 0:NB]).then_inc(copied, 1)
                v.wait_ge(summed, 1)
                c.link(v.tensor_copy(totals[:, :], ps_sums[:, P:P + NB]))
                c.link(v.tensor_tensor_scan(upto[:, :], totals[:, :], zeros[:, :], 0.0, ALU.add, ALU.add))
                c.link(v.tensor_tensor(upto[:, :], upto[:, :], totals[:, :], ALU.subtract))
                c.link(v.tensor_tensor(A.first[:, :], upto[:, :], ps_sums[:, 0:NB], ALU.add))

            @block.tensor
            def _(pe):
                pe.wait_ge(hot, 1)
                pe.matmul(ps_count[:, 0:NB], zeros_b[:, :], zeros_b[:, 0:NB], start=True, stop=True).then_inc(used, 1)
                with pe.Fori(0, NT // U) as i:
                    for k in range(U):
                        pe.wait_ge(hot, i * U + (k + 2))
                        m = pe.matmul(ps_count[:, 0:NB], onehot_lo[:, k, :], onehot_hi[:, k, :], start=False, stop=True,
                                      skip_group_check=True)
                    m.then_inc(used, 1)
                pe.wait_ge(copied, 1)
                pe.matmul(ps_sums[:, 0:NB], K.above[:, :], counts[:, :], start=True, stop=True)
                pe.matmul(ps_sums[:, P:P + NB], K.ones[:, :], counts[:, :], start=True, stop=True).then_inc(summed, 1)


def attention_vectors(nc, K, A, G, w_lin, b_lin, w_edge, b_edge, att, bias, edge_attr, T):
    with Stage(nc, "vectors") as s:
        side = s.sb("side", [D, HEADS, D + BOND + 2])
        att_c = s.sb("att_c", [D, HEADS, 2])
        att_b = s.sb("att_b", [D, HEADS, 2, P])
        vec = s.sb("vec", [P, HEADS, 2, D + BOND + 2])
        prod = s.sb("prod", [P, NB, D])
        node_z = s.sb("node_z", [P, NB, HEADS])
        attr = s.sb("attr", [P, NT, BOND])
        wb = s.sb("wb", [ROW, HEADS * D])
        const = s.sb("const", [P, HEADS])
        ps_vec = s.ps("ps_vec", [P, 512])
        loaded, chain, spread, multiplied, stored, padded = [s.sem(n) for n in ("loaded", "chain", "spread", "multiplied", "stored", "padded")]
        NL = 16 * (2 * HEADS + 2 + HEADS + 2 + 5 + 1)
        with nc.Block() as block:
            @block.sync
            def _(sp):
                sp.wait_ge(padded, 1)
                with nc.allow_non_contiguous_dma(reason="small transposed weights"):
                    for h in range(HEADS):
                        cols = slice(h * D, (h + 1) * D)
                        sp.dma_start(side[:, h, 0:D], w_lin[:, cols].rearrange("k d -> d k")).then_inc(loaded, 16)
                        sp.dma_start(side[:, h, D:D + BOND], w_edge[:, cols].rearrange("k d -> d k")).then_inc(loaded, 16)
                        sp.dma_start(att_c[:, h, :], att[0, h, :].rearrange("(s d) -> d s", s=2)).then_inc(loaded, 16)
                    sp.dma_start(side[:, :, D + BOND:D + BOND + 1], b_lin.rearrange("(h d o) -> d h o", d=D, o=1)).then_inc(loaded, 16)
                    sp.dma_start(side[:, :, D + BOND + 1:D + BOND + 2], b_edge.rearrange("(h d o) -> d h o", d=D, o=1)).then_inc(loaded, 16)
                sp.dma_start(attr[0:P - 1, :, :], edge_attr[0:(P - 1) * NT, :].rearrange("(p c) k -> p c k", c=NT)).then_inc(loaded, 16)
                sp.dma_start(attr[P - 1:P, 0:LASTC, :], edge_attr[(P - 1) * NT:E, :].rearrange("(p c) k -> p c k", p=1)).then_inc(loaded, 16)
                sp.dma_start(K.w_att[0:D, :], w_lin).then_inc(loaded, 16)
                sp.dma_start(K.w_att[C_ATTR:C_ONE, :], w_edge).then_inc(loaded, 16)
                sp.dma_start(K.w_att[C_ONE:ROW, :], b_lin.rearrange("(a n) -> a n", a=1)).then_inc(loaded, 16)
                sp.dma_start(wb[C_ONE:ROW, :], b_edge.rearrange("(a n) -> a n", a=1)).then_inc(loaded, 16)
                sp.dma_start(K.bias[:, :], bias.rearrange("(a n) -> a n", a=1).to_broadcast([P, D])).then_inc(loaded, 16)
                sp.dma_start(T.nodes[:, 0:D].rearrange("(b p) d -> p b d", p=P), K.x[:, :, :]).then_inc(loaded, 16)
                sp.wait_ge(stored, 1)
                sp.dma_start(T.nodes[:, D:D + HEADS].rearrange("(b p) d -> p b d", p=P), node_z[:, :, :]).then_inc(loaded, 16)
                sp.wait_ge(loaded, NL + 16)

            @block.vector
            def _(v):
                c = Chain(v, chain)
                v.memset(attr[:, :, :], 0.0)
                v.memset(K.w_att[:, :], 0.0)
                c.link(v.memset(wb[:, :], 0.0))
                v.sem_inc(padded, 1)
                v.wait_ge(loaded, NL)
                c.link(v.tensor_tensor(K.w_att[:, :], K.w_att[:, :], wb[:, :], ALU.add))
                for h in range(HEADS):
                    for e in range(2):
                        last = v.tensor_scalar(att_b[:, h, e, :], K.ones[0:D, :], att_c[:, h, e:e + 1], None, ALU.mult)
                last.then_inc(spread, 1)
                v.wait_ge(multiplied, 1)
                c.link(v.tensor_copy(vec[:, :, :, :], ps_vec[:, 0:HEADS * 2 * (D + BOND + 2)].rearrange("p (h e n) -> p h e n", h=HEADS, e=2)))
                bl, be = D + BOND, D + BOND + 1
                c.link(v.tensor_tensor(const[:, :], vec[:, :, 0, bl], vec[:, :, 1, bl], ALU.add))
                c.link(v.tensor_tensor(const[:, :], const[:, :], vec[:, :, 1, be], ALU.add))
                for h in range(HEADS):
                    for e in range(2):
                        c.link(v.tensor_tensor(prod[:, :, :], K.x[:, :, :], vec[:, h, e:e + 1, 0:D].to_broadcast([P, NB, D]), ALU.mult))
                        if e == 0:
                            c.link(v.tensor_reduce(A.s_node[:, h, :], prod[:, :, :], X_AXIS, ALU.add))
                            c.link(v.tensor_scalar(A.s_node[:, h, :], A.s_node[:, h, :], const[:, h:h + 1], None, ALU.add))
                        else:
                            c.link(v.tensor_reduce(node_z[:, :, h], prod[:, :, :], X_AXIS, ALU.add))
                v.sem_inc(stored, 1)
                for h in range(HEADS):
                    c.link(v.tensor_scalar(G.part[:, :, h], attr[:, :, 0], vec[:, h, 1, D:D + 1], None, ALU.mult))
                    for k in range(1, BOND):
                        c.link(v.scalar_tensor_tensor(G.part[:, :, h], attr[:, :, k], vec[:, h, 1, D + k:D + k + 1], G.part[:, :, h],
                                                      ALU.mult, ALU.add))
                v.tensor_copy(G.tail[:, :, 0], A.src_f[:, :])
                v.tensor_copy(G.tail[:, :, 1:1 + BOND], attr[:, :, :])
                v.memset(G.tail[:, :, 1 + BOND], 1.0)

            @block.tensor
            def _(pe):
                pe.wait_ge(spread, 1)
                n = D + BOND + 2
                for h in range(HEADS):
                    for e in range(2):
                        o = (2 * h + e) * n
                        m = pe.matmul(ps_vec[:, o:o + n], att_b[:, h, e, :], side[:, h, :], start=True, stop=True)
                m.then_inc(multiplied, 1)


HALF = U // 2


def sort_attention(nc, K, A, G, T):
    with Stage(nc, "sort") as s:
        hot_lo = s.sb("hot_lo", [P, U, P], BF16)
        hot_hi = s.sb("hot_hi", [P, U, NB], BF16)
        looked_up = s.sb("looked_up", [P, 2, P])
        places = s.sb("places", [P, 2, NB])
        junk_a = s.sb("junk_a", [P, U, P])
        junk_b = s.sb("junk_b", [P, U, 3, NB])
        rank = s.sb("rank", [P, U])
        found = s.sb("found", [P, 3, U])
        z = s.sb("z", [P, U, HEADS])
        pos = s.sb("pos", [P, U], I32)
        fetch = s.sb("fetch", [P, U], I32)
        rec = s.sb("rec", [P, U, ROWP])
        blank = s.sb("blank", [P, ROWP])
        ps_same = s.ps("ps_same", [P, 2, 512])
        ps_hot = s.ps("ps_hot", [P, 2, 1024], BF16)
        ps_find = s.ps("ps_find", [P, 2, 512])
        ps_place = s.ps("ps_place", [P, 512])
        names = ("chain", "hot", "same", "ranked", "turned", "turn_copied", "found_ready", "found_used", "updated",
                 "place_copied", "tail_ready", "rec_ready", "cleared", "fetch_ready")
        (chain, hot, same, ranked, turned, turn_copied, found_ready, found_used, updated,
         place_copied, tail_ready, rec_ready, cleared, fetch_ready) = [s.sem(n) for n in names]
        got = [s.pool_dma_sem(f"got{k}") for k in range(U)]
        sent = [s.pool_dma_sem(f"sent{k}") for k in range(U)]
        passed = s.sem("passed")
        with nc.Block() as block:
            @block.gpsimd
            def _(pool):
                pool.wait_ge(cleared, 1)
                for k in range(U):
                    pool.dma_start(rec[:, k, :], blank[:, :]).then_inc(sent[k], 16)
                with pool.Fori(0, NT // U) as i:
                    for k in range(U):
                        wait_apart(pool, passed, sent[k], i * 16 + 16)
                        if k % HALF == 0:
                            wait_apart(pool, passed, fetch_ready, i * 2 + (k // HALF + 1))
                        pool.indirect_dma_start(rec[:, k, 0:D + HEADS], None, T.nodes,
                                                bass.IndirectOffsetOnAxis(fetch[:, k:k + 1], axis=0)).then_inc(got[k], 16)
                    for half in range(2):
                        wait_apart(pool, passed, tail_ready, i * 2 + (half + 1))
                        wait_apart(pool, passed, rec_ready, i * 2 + (half + 1))
                        for k in range(half * HALF, (half + 1) * HALF):
                            pool.indirect_dma_start(T.sorted, bass.IndirectOffsetOnAxis(pos[:, k:k + 1], axis=0),
                                                    rec[:, k, :], None).then_inc(sent[k], 16)
                for k in range(U):
                    pool.wait_ge(sent[k], 16 * (NT // U + 1))

            @block.vector
            def _(v):
                c = Chain(v, chain)
                v.memset(blank[:, :], 0.0).then_inc(cleared, 1)
                v.sem_inc(ranked, 2)
                v.sem_inc(found_used, 2)
                with v.Fori(0, NT // U) as i:
                    t0 = i * U
                    v.wait_ge(found_used, t0 + 2)
                    for k in range(U):
                        v.wait_ge(updated, t0 + (k + 1))
                        v.tensor_scalar(hot_lo[:, k, :], K.iota_b[:, :], A.lo_f[:, at(t0 + k)], None, ALU.is_equal)
                        v.tensor_scalar(hot_hi[:, k, :], K.iota_b[:, 0:NB], A.hi_f[:, at(t0 + k)], None,
                                        ALU.is_equal).then_inc(hot, 1)
                    v.wait_ge(hot, t0 + U)
                    for half in range(2):
                        ks = slice(half * HALF, (half + 1) * HALF)
                        for k in range(half * HALF, (half + 1) * HALF):
                            v.wait_ge(same, t0 + (k + 1))
                            v.scalar_tensor_tensor(junk_a[:, k, :], ps_same[:, k % 2, 0:P], A.src_f[:, at(t0 + k)], K.below[:, :],
                                                   ALU.is_equal, ALU.mult, accum_out=rank[:, k:k + 1]).then_inc(ranked, 1)
                            v.wait_ge(found_ready, t0 + (k + 3))
                            for j in range(3):
                                m = v.scalar_tensor_tensor(junk_b[:, k, j, :], ps_find[:, k % 2, j * NB:(j + 1) * NB], 1.0,
                                                           hot_hi[:, k, :], ALU.mult, ALU.mult, accum_out=found[:, j, k:k + 1])
                            m.then_inc(found_used, 1)
                        v.wait_ge(found_used, t0 + ((half + 1) * HALF + 2))
                        for k in range(half * HALF, (half + 1) * HALF):
                            v.wait_ge(sent[k], i * 16 + 16)
                        v.tensor_tensor(pos[:, ks], found[:, 0, ks], rank[:, ks], ALU.add)
                        v.tensor_tensor(z[:, ks, :], found[:, 1:3, ks].rearrange("p h k -> p k h"),
                                        G.part[:, bass.ds(t0 + half * HALF, HALF), :], ALU.add).then_inc(chain, 1)
                        v.wait_ge(chain, i * 2 + (half + 1))
                        for k in range(half * HALF, (half + 1) * HALF):
                            v.wait_ge(got[k], i * 16 + 16)
                        v.tensor_tensor(rec[:, ks, C_Z:C_KEY], rec[:, ks, C_Z:C_KEY], z[:, ks, :], ALU.add).then_inc(rec_ready, 1)

            @block.scalar
            def _(act):
                act.copy(places[:, 0, :], A.first[:, :]).then_inc(place_copied, 1)
                act.sem_inc(turn_copied, 2)
                for half in range(2):
                    ks = slice(half * HALF, (half + 1) * HALF)
                    act.copy(fetch[:, ks], A.dst_i[:, ks]).then_inc(fetch_ready, 1)
                with act.Fori(0, NT // U) as i:
                    t0 = i * U
                    for half in range(2):
                        ks = slice(half * HALF, (half + 1) * HALF)
                        for k in range(half * HALF, (half + 1) * HALF):
                            act.wait_ge(sent[k], i * 16 + 16)
                        act.copy(rec[:, ks, C_KEY:ROW], G.tail[:, bass.ds(t0 + half * HALF, HALF), :]).then_inc(tail_ready, 1)
                        for k in range(half * HALF, (half + 1) * HALF):
                            act.wait_ge(turned, t0 + (k + 1))
                            act.wait_ge(found_ready, t0 + (k + 1))
                            act.copy(looked_up[:, k % 2, :], ps_hot[:, k % 2, 0:P]).then_inc(turn_copied, 1)
                            act.wait_ge(updated, t0 + (U + k + 1))
                            act.wait_ge(found_ready, t0 + (k + 2))
                            act.copy(places[:, (k + 1) % 2, :], ps_place[:, 0:NB]).then_inc(place_copied, 1)
                        for k in range(half * HALF, (half + 1) * HALF):
                            act.wait_ge(got[k], i * 16 + 16)
                        act.copy(fetch[:, ks], A.dst_i[:, bass.ds(t0 + (U + half * HALF), HALF)]).then_inc(fetch_ready, 1)

            @block.tensor
            def _(pe):
                pe.sem_inc(found_ready, 2)
                pe.matmul(ps_place[:, 0:NB], K.ident[:, :], A.first[:, :], start=True, stop=True).then_inc(updated, U)
                with pe.Fori(0, NT // U) as i:
                    t0 = i * U
                    for k in range(U):
                        pe.wait_ge(hot, t0 + (k + 1))
                        pe.wait_ge(ranked, t0 + (k + 1))
                        pe.matmul(ps_same[:, k % 2, 0:P], A.hi[:, at(t0 + k)].to_broadcast([P, P]), K.ident_128[:, :],
                                  start=True, stop=False)
                        pe.matmul(ps_same[:, k % 2, 0:P], A.lo[:, at(t0 + k)].to_broadcast([P, P]), K.ident_b[:, :],
                                  start=False, stop=True).then_inc(same, 1)
                        pe.wait_ge(turn_copied, t0 + (k + 1))
                        pe.transpose(ps_hot[:, k % 2, 0:P], hot_lo[:, k, :], K.ident_b[:, :]).then_inc(turned, 1)
                        pe.wait_ge(place_copied, t0 + (k + 1))
                        pe.matmul(ps_place[:, 0:NB], hot_lo[:, k, :], hot_hi[:, k, :], start=False, stop=True,
                                  skip_group_check=True).then_inc(updated, 1)
                        pe.wait_ge(turn_copied, t0 + (k + 3))
                        pe.wait_ge(found_used, t0 + (k + 1))
                        pe.matmul(ps_find[:, k % 2, 0:NB], looked_up[:, k % 2, :], places[:, k % 2, :], start=True, stop=True)
                        pe.matmul(ps_find[:, k % 2, NB:3 * NB], looked_up[:, k % 2, :],
                                  A.s_node[:, :, :].rearrange("p h b -> p (h b)"), start=True, stop=True).then_inc(found_ready, 1)


def softmax_weights(nc, K, T, M):
    with Stage(nc, "soft") as s:
        zk = s.sb("zk", [P, NT, HEADS + 1])
        key = s.sb("key", [P, NT])
        skip = s.sb("skip", [P, NT])
        skip_b = s.sb("skip_b", [P, NT])
        most = s.sb("most", [P, HEADS, NT])
        leaky = s.sb("leaky", [P, HEADS, NT])
        scratch = s.sb("scratch", [P, HEADS, NT])
        edge = s.sb("edge", [P, 6])
        row = s.sb("row", [1, 6, P])
        r = s.sb("r", [1, 8, P])
        carry_r = s.sb("carry_r", [1, 4, P])
        carry = s.sb("carry", [P, 4])
        loaded, chain, ends, turned, carried, brought, ready, raised, stored = [
            s.sem(n) for n in ("loaded", "chain", "ends", "turned", "carried", "brought", "ready", "raised", "stored")]
        with nc.Block() as block:
            @block.sync
            def _(sp):
                sp.dma_start(zk[:, :, :], T.sorted[:, C_Z:C_KEY + 1].rearrange("(p c) w -> p c w", c=NT)).then_inc(loaded, 16)
                sp.wait_ge(ends, 1)
                with nc.allow_non_contiguous_dma(reason="a column of 128 words becomes a row"):
                    for j in range(6):
                        sp.dma_start(row[0:1, j, :], edge[:, j:j + 1]).then_inc(turned, 16)
                    sp.wait_ge(carried, 1)
                    for j in range(4):
                        sp.dma_start(carry[:, j:j + 1], carry_r[0:1, j, :]).then_inc(brought, 16)
                sp.wait_ge(raised, 1)
                sp.dma_start(M.key.rearrange("(p c) -> p c", c=NT), key[:, :]).then_inc(stored, 16)
                for h in range(HEADS):
                    sp.dma_start(M.e[h].rearrange("(p c) -> p c", c=NT), scratch[:, h, :]).then_inc(stored, 16)
                sp.wait_ge(stored, 16 * (1 + HEADS))

            @block.vector
            def _(v):
                c = Chain(v, chain)
                v.wait_ge(loaded, 16)
                c.link(v.tensor_copy(key[:, :], zk[:, :, HEADS]))
                v.memset(skip[:, 0:1], LOW)
                v.memset(skip_b[:, NT - 1:NT], LOW)
                v.tensor_scalar(edge[:, 0:1], key[:, 0:1], 1.0, None, ALU.mult)
                v.tensor_scalar(edge[:, 1:2], key[:, NT - 1:NT], 1.0, None, ALU.mult)
                c.link(v.tensor_tensor(skip[:, 1:NT], key[:, 1:NT], key[:, 0:NT - 1], ALU.not_equal))
                c.link(v.tensor_scalar(skip[:, 1:NT], skip[:, 1:NT], LOW, None, ALU.mult))
                c.link(v.tensor_copy(skip_b[:, 0:NT - 1], skip[:, 1:NT]))
                for h in range(HEADS):
                    c.link(v.tensor_tensor_scan(scratch[:, h, :], skip[:, :], zk[:, :, h], 0.0, ALU.add, ALU.max))
                    c.link(v.tensor_tensor_scan(most[:, h, ::-1], skip_b[:, ::-1], scratch[:, h, ::-1], 0.0, ALU.add, ALU.max))
                    v.tensor_copy(edge[:, 2 + h:3 + h], most[:, h, 0:1])
                    c.link(v.tensor_copy(edge[:, 4 + h:5 + h], most[:, h, NT - 1:NT]))
                v.sem_inc(ends, 1)
                v.wait_ge(turned, 96)
                c.link(v.memset(r[:, :, :], LOW))
                v.tensor_tensor(r[0:1, 0, 1:P], row[0:1, 0, 1:P], row[0:1, 1, 0:P - 1], ALU.not_equal)
                c.link(v.tensor_tensor(r[0:1, 1, :], row[0:1, 0, :], row[0:1, 1, :], ALU.not_equal))
                v.tensor_scalar(r[0:1, 0, 1:P], r[0:1, 0, 1:P], LOW, None, ALU.mult)
                c.link(v.tensor_scalar(r[0:1, 1, :], r[0:1, 1, :], LOW, None, ALU.mult))
                v.tensor_tensor(r[0:1, 2, :], r[0:1, 0, :], r[0:1, 1, :], ALU.min)
                c.link(v.tensor_tensor(r[0:1, 3, 0:P - 1], r[0:1, 0, 1:P], r[0:1, 1, 0:P - 1], ALU.min))
                c.link(v.memset(carry_r[:, :, :], LOW))
                for h in range(HEADS):
                    v.tensor_tensor_scan(r[0:1, 4 + h, :], r[0:1, 2, :], row[0:1, 4 + h, :], 0.0, ALU.add, ALU.max)
                    c.link(v.tensor_tensor_scan(r[0:1, 6 + h, ::-1], r[0:1, 3, ::-1], row[0:1, 2 + h, ::-1], 0.0, ALU.add, ALU.max))
                    v.tensor_tensor(carry_r[0:1, h, 1:P], r[0:1, 4 + h, 0:P - 1], r[0:1, 0, 1:P], ALU.add)
                    c.link(v.tensor_tensor(carry_r[0:1, 2 + h, 0:P - 1], r[0:1, 6 + h, 1:P], r[0:1, 0, 1:P], ALU.add))
                v.sem_inc(carried, 1)
                v.wait_ge(brought, 64)
                v.tensor_scalar(skip[:, :], key[:, :], edge[:, 0:1], LOW, ALU.not_equal, ALU.mult)
                c.link(v.tensor_scalar(skip_b[:, :], key[:, :], edge[:, 1:2], LOW, ALU.not_equal, ALU.mult))
                for h in range(HEADS):
                    c.link(v.scalar_tensor_tensor(most[:, h, :], skip[:, :], carry[:, h:h + 1], most[:, h, :], ALU.add, ALU.max))
                    c.link(v.scalar_tensor_tensor(most[:, h, :], skip_b[:, :], carry[:, 2 + h:3 + h], most[:, h, :], ALU.add, ALU.max))
                    v.scalar_tensor_tensor(leaky[:, h, :], zk[:, :, h], NEG_SLOPE, zk[:, :, h], ALU.mult, ALU.max)
                    c.link(v.scalar_tensor_tensor(scratch[:, h, :], most[:, h, :], NEG_SLOPE, most[:, h, :], ALU.mult, ALU.max))
                    c.link(v.tensor_tensor(leaky[:, h, :], leaky[:, h, :], scratch[:, h, :], ALU.subtract))
                v.sem_inc(ready, 1)

            @block.scalar
            def _(act):
                act.wait_ge(ready, 1)
                act.activation(scratch[:, :, :], leaky[:, :, :], ACT.Exp).then_inc(raised, 1)


def make_visits(nc, K, T, name, keys, block_row, tile_row, where, others):
    sources = [keys] + [a for a, _ in others]
    targets = [where] + [b for _, b in others]
    with Stage(nc, name) as s:
        last = s.sb("last", [P, GT])
        before = s.sb("before", [P, NB, GT])
        tiles = s.sb("tiles", [P, NB])
        start = s.sb("start", [P, NB])
        begun = s.sb("begun", [P, GV, NB])
        blk = s.sb("blk", [P, GV])
        tile = s.sb("tile", [P, GV])
        blk_i = s.sb("blk_i", [P, GV], I32)
        tile_i = s.sb("tile_i", [P, GV], I32)
        rows = s.sb("rows", [P, 2, P])
        rel = s.sb("rel", [P, 2, P])
        minus = s.sb("minus", [P, GV])
        ps_tiles = s.ps("ps_tiles", [P, 512])
        ps_rows = s.ps("ps_rows", [P, 2, 512])
        loaded, chain, partial, summed, indexed, kept, kept2, shifted, turned, copied = [
            s.sem(n) for n in ("loaded", "chain", "partial", "summed", "indexed", "kept", "kept2", "shifted", "turned", "copied")]
        got = [s.pool_dma_sem(f"got{k}") for k in range(2)]
        jobs = [(j, g) for j in range(len(sources)) for g in range(GV)]
        with nc.Block() as block:
            @block.sync
            def _(sp):
                with nc.allow_non_contiguous_dma(reason="one key of each tile, and tables of a word per visit"):
                    sp.dma_start(last[:, :], keys.rearrange("(g p e) -> p g e", p=P, e=P)[:, :, P - 1:P]).then_inc(loaded, 16)
                    sp.wait_ge(indexed, 1)
                    sp.dma_start(T.blk.rearrange("(g p) -> p g", p=P), blk_i[:, :]).then_inc(kept, 16)
                    sp.dma_start(T.tile.rearrange("(g p) -> p g", p=P), tile_i[:, :]).then_inc(kept, 16)
                sp.wait_ge(kept, 32)
                sp.dma_start(block_row[0:1, :], T.blk.rearrange("(a v) -> a v", a=1)).then_inc(kept2, 16)
                sp.dma_start(tile_row[0:1, :], T.tile.rearrange("(a v) -> a v", a=1)).then_inc(kept2, 16)
                sp.wait_ge(kept2, 32)

            @block.gpsimd
            def _(pool):
                pool.wait_ge(indexed, 1)
                for n, (j, g) in enumerate(jobs):
                    if n >= 2:
                        pool.wait_ge(shifted, n - 1)
                    pool.indirect_dma_start(rows[:, n % 2, :], None, sources[j].rearrange("(t e) -> t e", e=P),
                                            bass.IndirectOffsetOnAxis(tile_i[:, g:g + 1], axis=0)).then_inc(got[n % 2], 16)

            @block.vector
            def _(v):
                c = Chain(v, chain)
                v.wait_ge(loaded, 16)
                for g in range(GT):
                    m = v.tensor_scalar(before[:, :, g], K.edges[:, :], last[:, g:g + 1], None, ALU.is_gt)
                c.link(m)
                v.tensor_reduce(tiles[:, :], before[:, :, :], X_AXIS, ALU.add).then_inc(partial, 1)
                v.wait_ge(summed, 1)
                c.link(v.scalar_tensor_tensor(start[:, :], K.edges[:, :], 1.0 / P, ps_tiles[:, 0:NB], ALU.mult, ALU.add))
                c.link(v.memset(start[:, NB - 1:NB], float(VISITS)))
                for g in range(GV):
                    m = v.tensor_scalar(begun[:, g, :], start[:, :], K.visit[:, g:g + 1], None, ALU.is_le)
                c.link(m)
                c.link(v.tensor_reduce(blk[:, :], begun[:, :, :], X_AXIS, ALU.add))
                c.link(v.tensor_tensor(tile[:, :], K.visit[:, :], blk[:, :], ALU.subtract))
                c.link(v.tensor_scalar(tile[:, :], tile[:, :], float(NT - 1), None, ALU.min))
                v.tensor_copy(blk_i[:, :], blk[:, :])
                v.tensor_scalar(minus[:, :], blk[:, :], -float(P), None, ALU.mult)
                c.link(v.tensor_copy(tile_i[:, :], tile[:, :]))
                v.sem_inc(indexed, 1)
                for n, (j, g) in enumerate(jobs):
                    v.wait_ge(got[n % 2], 16 * (n // 2 + 1))
                    if n >= 2:
                        v.wait_ge(turned, n - 1)
                    if j == 0:
                        v.tensor_scalar(rel[:, n % 2, :], rows[:, n % 2, :], minus[:, g:g + 1], None, ALU.add).then_inc(shifted, 1)
                    else:
                        v.tensor_copy(rel[:, n % 2, :], rows[:, n % 2, :]).then_inc(shifted, 1)

            @block.tensor
            def _(pe):
                pe.wait_ge(partial, 1)
                pe.matmul(ps_tiles[:, 0:NB], K.ones[:, :], tiles[:, :], start=True, stop=True).then_inc(summed, 1)
                for n in range(len(jobs)):
                    pe.wait_ge(shifted, n + 1)
                    if n >= 2:
                        pe.wait_ge(copied, n - 1)
                    pe.transpose(ps_rows[:, n % 2, 0:P], rel[:, n % 2, :], K.ident[:, :]).then_inc(turned, 1)

            @block.scalar
            def _(act):
                for n, (j, g) in enumerate(jobs):
                    act.wait_ge(turned, n + 1)
                    act.copy(targets[j][:, g * P:(g + 1) * P], ps_rows[:, n % 2, 0:P]).then_inc(copied, 1)


REASON = "the table's values are blocks 0 to NB and tiles 0 to NT - 1 by construction"


def sum_attention(nc, K, T, V, total):
    with Stage(nc, "att") as s:
        rows = s.sb("rows", [P, U, ROWP])
        hot = s.sb("hot", [P, U, P])
        scaled = s.sb("scaled", [P, U, HEADS, P])
        ps = s.ps("ps", [P, U // 2, 512])
        built, weighed, multiplied, added = [s.sem(n) for n in ("built", "weighed", "multiplied", "added")]
        got = [s.sem(f"got{k}") for k in range(U)]
        W = HEADS * ROW

        def bank(k):
            return ps[:, k // 2, (k % 2) * W:(k % 2 + 1) * W]

        with nc.Block() as block:
            @block.sync
            def _(sp):
                with sp.Fori(0, NV // U) as i:
                    tiles = load_registers(nc, mybir.EngineType.SP, V.tile_row, i, NT - 1, REASON)
                    for k in range(U):
                        sp.wait_ge(multiplied, i * U + (k + 1))
                        sp.dma_start(rows[:, k, :], T.sorted[bass.ds(tiles[k] * P, P), :]).then_inc(got[k], 16)

            @block.vector
            def _(v):
                v.memset(total[:, :, :, :], 0.0).then_inc(added, 1)
                with v.Fori(0, NV // U) as i:
                    blocks = load_registers(nc, mybir.EngineType.DVE, V.block_row, i, NB, REASON)
                    for k in range(U):
                        v.wait_ge(weighed, i * U + (k + 1))
                        v.tensor_scalar(hot[:, k, :], K.iota[:, :], V.rel[:, at(i * U + k)], None, ALU.is_equal).then_inc(built, 1)
                    for k in range(U):
                        v.wait_ge(multiplied, i * U + (U + (k | 1) + 1))
                        v.wait_ge(added, i * U + (k + 1))
                        t = total[:, bass.ds(blocks[k], 1), :, :].rearrange("p o h w -> p (o h w)")
                        v.tensor_tensor(t, t, bank(k), ALU.add).then_inc(added, 1)

            @block.scalar
            def _(act):
                act.sem_inc(weighed, U)
                with act.Fori(0, NV // U) as i:
                    for k in range(U):
                        act.wait_ge(built, i * U + (k + 1))
                        act.wait_ge(multiplied, i * U + (k + 1))
                        for h in range(HEADS):
                            m = act.activation(scaled[:, k, h, :], hot[:, k, :], ACT.Copy, scale=V.e[h][:, at(i * U + k)])
                        m.then_inc(weighed, 1)

            @block.tensor
            def _(pe):
                pe.sem_inc(multiplied, U)
                with pe.Fori(0, NV // U) as i:
                    for k in range(U):
                        pe.wait_ge(weighed, i * U + (U + k + 1))
                        pe.wait_ge(got[k], i * 16 + 16)
                        if k == 0:
                            pe.wait_ge(added, i * U + 1)
                        for h in range(HEADS):
                            m = pe.matmul(bank(k)[:, h * ROW:(h + 1) * ROW], scaled[:, k, h, :], rows[:, k, 0:ROW], start=True, stop=True)
                        m.then_inc(multiplied, 1)


def finish_attention(nc, K, total):
    with Stage(nc, "proj") as s:
        inv = s.sb("inv", [P, NB, HEADS])
        held = s.sb("held", [P, 2, HEADS, ROW])
        turned = s.sb("turned", [ROW, 2, HEADS, P])
        ps_turn = s.ps("ps_turn", [ROW, 2, 512])
        ps_out = s.ps("ps_out", [P, 2, 512])
        chain, scaled, flipped, copied, projected, added = [
            s.sem(n) for n in ("chain", "scaled", "flipped", "copied", "projected", "added")]
        with nc.Block() as block:
            @block.vector
            def _(v):
                c = Chain(v, chain)
                c.link(v.tensor_scalar(inv[:, :, :], total[:, 0:NB, :, C_ONE], 1e-16, 1.0 / 0.5, ALU.add, ALU.mult))
                c.link(v.reciprocal(inv[:, :, :], inv[:, :, :]))
                c.link(v.tensor_tensor(K.x[:, :, :], K.x[:, :, :], K.bias[:, :].rearrange("p (o d) -> p o d", o=1).to_broadcast([P, NB, D]), ALU.add))
                v.sem_inc(added, 2)
                with v.Fori(0, NB // 2) as i:
                    for k in range(2):
                        v.wait_ge(flipped, i * 2 + (k + 1))
                        for h in range(HEADS):
                            m = v.tensor_scalar(held[:, k, h, :], total[:, bass.ds(i * 2 + k, 1), h, :].rearrange("p o w -> p (o w)"),
                                                inv[:, bass.ds(i * 2 + k, 1), h], None, ALU.mult)
                        m.then_inc(scaled, 1)
                    for k in range(2):
                        v.wait_ge(projected, i * 2 + (k + 3))
                        xb = K.x[:, bass.ds(i * 2 + k, 1), :].rearrange("p o d -> p (o d)")
                        v.tensor_tensor(xb, xb, ps_out[:, k, 0:D], ALU.add).then_inc(added, 1)

            @block.tensor
            def _(pe):
                pe.sem_inc(projected, 2)
                pe.sem_inc(flipped, 2)
                with pe.Fori(0, NB // 2) as i:
                    for k in range(2):
                        pe.wait_ge(copied, i * 2 + (k + 1))
                        pe.wait_ge(scaled, i * 2 + (k + 1))
                        for h in range(HEADS):
                            m = pe.transpose(ps_turn[:, k, h * P:(h + 1) * P], held[:, k, h, :], K.ident[:, :])
                        m.then_inc(flipped, 1)
                    for k in range(2):
                        pe.wait_ge(copied, i * 2 + (k + 3))
                        pe.wait_ge(added, i * 2 + (k + 1))
                        for h in range(HEADS):
                            m = pe.matmul(ps_out[:, k, 0:D], turned[:, k, h, :], K.w_att[:, h * D:(h + 1) * D],
                                          start=(h == 0), stop=(h == HEADS - 1))
                        m.then_inc(projected, 1)

            @block.scalar
            def _(act):
                act.sem_inc(copied, 2)
                with act.Fori(0, NB // 2) as i:
                    for k in range(2):
                        act.wait_ge(flipped, i * 2 + (k + 3))
                        act.wait_ge(projected, i * 2 + (k + 1))
                        act.copy(turned[:, k, :, :].rearrange("w h p -> w (h p)"), ps_turn[:, k, 0:HEADS * P]).then_inc(copied, 1)


def layer_norm(nc, K, name, addend=None):
    with Stage(nc, name) as s:
        sq = s.sb("sq", [P, NB, D])
        mean = s.sb("mean", [P, NB])
        var = s.sb("var", [P, NB])
        chain, ready, rooted = [s.sem(n) for n in ("chain", "ready", "rooted")]

        def wide(a):
            return a[:, :].rearrange("p (b o) -> p b o", o=1).to_broadcast([P, NB, D])

        with nc.Block() as block:
            @block.vector
            def _(v):
                c = Chain(v, chain)
                x = K.x[:, :, :]
                if addend is not None:
                    c.link(v.tensor_tensor(x, x, addend, ALU.add))
                c.link(v.tensor_reduce(mean[:, :], x, X_AXIS, ALU.add))
                c.link(v.tensor_scalar(mean[:, :], mean[:, :], 1.0 / D, None, ALU.mult))
                c.link(v.tensor_tensor(x, x, wide(mean), ALU.subtract))
                c.link(v.tensor_tensor(sq[:, :, :], x, x, ALU.mult))
                c.link(v.tensor_reduce(var[:, :], sq[:, :, :], X_AXIS, ALU.add))
                c.link(v.tensor_scalar(var[:, :], var[:, :], 1.0 / D, EPS, ALU.mult, ALU.add))
                v.sem_inc(ready, 1)
                v.wait_ge(rooted, 1)
                c.link(v.reciprocal(var[:, :], var[:, :]))
                c.link(v.tensor_tensor(x, x, wide(var), ALU.mult))

            @block.scalar
            def _(act):
                act.wait_ge(ready, 1)
                act.activation(var[:, :], var[:, :], ACT.Sqrt).then_inc(rooted, 1)


def relation_table(nc, K, T, w_rel):
    H = RELS * D // 2
    with Stage(nc, "rel") as s:
        w = s.sb("w", [D, RELS, D])
        xt = s.sb("xt", [D, 2, P])
        held = s.sb("held", [P, 2, D])
        y = s.sb("y", [P, 2, 2 * H])
        ps_x = s.ps("ps_x", [D, 2, 512])
        ps_y = s.ps("ps_y", [P, 2, 2, 512])
        loaded, staged, flipped, copied, multiplied, half_a, half_b = [
            s.sem(n) for n in ("loaded", "staged", "flipped", "copied", "multiplied", "half_a", "half_b")]
        stored = [s.sem(f"stored{k}") for k in range(2)]
        passed = s.sem("passed")
        with nc.Block() as block:
            @block.sync
            def _(sp):
                sp.dma_start(w[:, :, :], w_rel.rearrange("r k d -> k r d")).then_inc(loaded, 16)
                for k in range(2):
                    sp.dma_start(T.blank[k:k + 1, :], K.ones[0:1, 0:P]).then_inc(stored[k], 16)
                with sp.Fori(0, NB // 2) as i:
                    for k in range(2):
                        sp.wait_ge(half_a, i * 2 + (k + 3))
                        sp.wait_ge(half_b, i * 2 + (k + 3))
                        sp.dma_start(T.rel[bass.ds((i * 2 + k) * P, P), :], y[:, k, :]).then_inc(stored[k], 16)
                for k in range(2):
                    sp.wait_ge(stored[k], 16 * (NB // 2 + 1))

            @block.gpsimd
            def _(pool):
                with pool.Fori(0, NB // 2) as i:
                    for k in range(2):
                        pool.wait_ge(flipped, i * 2 + (k + 1))
                        pool.tensor_copy(held[:, k, :], K.x[:, bass.ds(i * 2 + k, 1), :].rearrange("p o d -> p (o d)")).then_inc(staged, 1)

            @block.tensor
            def _(pe):
                pe.wait_ge(loaded, 16)
                pe.sem_inc(multiplied, 2)
                pe.sem_inc(flipped, 2)
                with pe.Fori(0, NB // 2) as i:
                    for k in range(2):
                        wait_apart(pe, passed, copied, i * 2 + (k + 1))
                        wait_apart(pe, passed, staged, i * 2 + (k + 1))
                        pe.transpose(ps_x[:, k, 0:P], held[:, k, :], K.ident[:, :]).then_inc(flipped, 1)
                    for k in range(2):
                        pe.wait_ge(copied, i * 2 + (k + 3))
                        pe.wait_ge(half_a, i * 2 + (k + 1))
                        pe.wait_ge(half_b, i * 2 + (k + 1))
                        for half in range(2):
                            m = pe.matmul(ps_y[:, k, half, :], xt[:, k, :], w[:, half * (RELS // 2):(half + 1) * (RELS // 2), :].rearrange("k r d -> k (r d)"),
                                          start=True, stop=True)
                        m.then_inc(multiplied, 1)

            @block.scalar
            def _(act):
                act.sem_inc(copied, 2)
                act.sem_inc(half_a, 2)
                with act.Fori(0, NB // 2) as i:
                    for k in range(2):
                        act.wait_ge(flipped, i * 2 + (k + 3))
                        act.wait_ge(multiplied, i * 2 + (k + 1))
                        act.copy(xt[:, k, :], ps_x[:, k, 0:P]).then_inc(copied, 1)
                    for k in range(2):
                        act.wait_ge(multiplied, i * 2 + (k + 3))
                        act.wait_ge(stored[k], i * 16 + 16)
                        act.copy(y[:, k, 0:H], ps_y[:, k, 0, :]).then_inc(half_a, 1)

            @block.vector
            def _(v):
                v.sem_inc(half_b, 2)
                with v.Fori(0, NB // 2) as i:
                    for k in range(2):
                        v.wait_ge(multiplied, i * 2 + (k + 3))
                        v.wait_ge(stored[k], i * 16 + 16)
                        v.tensor_copy(y[:, k, H:2 * H], ps_y[:, k, 1, :]).then_inc(half_b, 1)


def node_table(nc, K, name, table):
    with Stage(nc, name) as s:
        stored = s.sem("stored")
        with nc.Block() as block:
            @block.sync
            def _(sp):
                sp.dma_start(table.rearrange("(b p) d -> p b d", p=P), K.x[:, :, :]).then_inc(stored, 16)
                sp.wait_ge(stored, 16)


def turn_nodes(nc, K, xt):
    with Stage(nc, "turn") as s:
        ps = s.ps("ps", [D, 2, 512])
        held = s.sb("held", [P, 2, D])
        staged, flipped, copied = s.sem("staged"), s.sem("flipped"), s.sem("copied")
        passed = s.sem("passed")
        with nc.Block() as block:
            @block.gpsimd
            def _(pool):
                with pool.Fori(0, NB // 2) as i:
                    for k in range(2):
                        pool.wait_ge(flipped, i * 2 + (k + 1))
                        pool.tensor_copy(held[:, k, :], K.x[:, bass.ds(i * 2 + k, 1), :].rearrange("p o d -> p (o d)")).then_inc(staged, 1)

            @block.tensor
            def _(pe):
                pe.sem_inc(flipped, 2)
                with pe.Fori(0, NB // 2) as i:
                    for k in range(2):
                        wait_apart(pe, passed, copied, i * 2 + (k + 1))
                        wait_apart(pe, passed, staged, i * 2 + (k + 1))
                        pe.transpose(ps[:, k, 0:P], held[:, k, :], K.ident[:, :]).then_inc(flipped, 1)

            @block.scalar
            def _(act):
                act.sem_inc(copied, 2)
                with act.Fori(0, NB // 2) as i:
                    for k in range(2):
                        act.wait_ge(flipped, i * 2 + (k + 3))
                        act.copy(xt[:, bass.ds((i * 2 + k) * P, P)], ps[:, k, 0:P]).then_inc(copied, 1)

            @block.vector
            def _(v):
                v.memset(xt[:, NP:NP + P], 0.0)


def sum_rows(nc, K, V, name, table, index, total, weight=None, xt=None):
    with Stage(nc, name) as s:
        rows = s.sb("rows", [P, U, D])
        fetch = s.sb("fetch", [P, U], I32)
        hot = s.sb("hot", [P, U, P])
        rows_t = s.sb("rows_t", [D, U, P])
        ps_sum = s.ps("ps_sum", [P, 2, 512])
        ps_turn = s.ps("ps_turn", [D, 2, 512])
        ps_dot = s.ps("ps_dot", [P, 2, 512])
        fetch_ready, built, multiplied, added, turned, copied, dotted = [
            s.sem(n) for n in ("fetch_ready", "built", "multiplied", "added", "turned", "copied", "dotted")]
        got = [s.pool_dma_sem(f"got{k}") for k in range(U)]

        def part(k):
            return ps_sum[:, k // HALF, (k % HALF) * D:(k % HALF + 1) * D]

        passed = s.sem("passed")
        with nc.Block() as block:
            @block.gpsimd
            def _(pool):
                with pool.Fori(0, NV // U) as i:
                    for k in range(U):
                        if k % HALF == 0:
                            wait_apart(pool, passed, fetch_ready, i * 2 + (k // HALF + 1))
                        wait_apart(pool, passed, multiplied, i * U + (k + 1))
                        pool.indirect_dma_start(rows[:, k, :], None, table,
                                                bass.IndirectOffsetOnAxis(fetch[:, k:k + 1], axis=0)).then_inc(got[k], 16)

            @block.scalar
            def _(act):
                for half in range(2):
                    ks = slice(half * HALF, (half + 1) * HALF)
                    act.copy(fetch[:, ks], index[:, ks]).then_inc(fetch_ready, 1)
                with act.Fori(0, NV // U) as i:
                    for half in range(2):
                        ks = slice(half * HALF, (half + 1) * HALF)
                        for k in range(half * HALF, (half + 1) * HALF):
                            act.wait_ge(got[k], i * 16 + 16)
                        act.copy(fetch[:, ks], index[:, bass.ds(i * U + (U + half * HALF), HALF)]).then_inc(fetch_ready, 1)
                        if xt is not None:
                            act.wait_ge(turned, i * 2 + (half + 1))
                            act.wait_ge(multiplied, i * U + (half + 1) * HALF)
                            act.copy(rows_t[:, ks, :].rearrange("d k e -> d (k e)"), ps_turn[:, half, :]).then_inc(copied, 1)

            @block.vector
            def _(v):
                v.memset(total[:, :, :], 0.0).then_inc(added, 1)
                with v.Fori(0, NV // U) as i:
                    blocks = load_registers(nc, mybir.EngineType.DVE, V.block_row, i, NB, REASON)
                    for half in range(2):
                        for k in range(half * HALF, (half + 1) * HALF):
                            v.wait_ge(multiplied, i * U + (k + 1))
                            rel = V.rel[:, at(i * U + k)]
                            if xt is not None:
                                v.wait_ge(dotted, i * U + (half + 1) * HALF)
                                m = v.scalar_tensor_tensor(hot[:, k, :], K.iota[:, :], rel, ps_dot[:, half, (k % HALF) * P:(k % HALF + 1) * P],
                                                           ALU.is_equal, ALU.mult)
                            elif weight is not None:
                                m = v.tensor_scalar(hot[:, k, :], K.iota[:, :], rel, weight[:, at(i * U + k)], ALU.is_equal, ALU.mult)
                            else:
                                m = v.tensor_scalar(hot[:, k, :], K.iota[:, :], rel, None, ALU.is_equal)
                            m.then_inc(built, 1)
                        for k in range(half * HALF, (half + 1) * HALF):
                            v.wait_ge(multiplied, i * U + (U + (half + 1) * HALF))
                            v.wait_ge(added, i * U + (k + 1))
                            t = total[:, bass.ds(blocks[k], 1), :].rearrange("p o d -> p (o d)")
                            v.tensor_tensor(t, t, part(k), ALU.add).then_inc(added, 1)

            @block.tensor
            def _(pe):
                pe.sem_inc(multiplied, U)
                with pe.Fori(0, NV // U) as i:
                    if xt is not None:
                        blocks = load_registers(nc, mybir.EngineType.PE, V.block_row, i, NB, REASON)
                    for half in range(2):
                        for k in range(half * HALF, (half + 1) * HALF):
                            wait_apart(pe, passed, got[k], i * 16 + 16)
                            if xt is not None:
                                if k % HALF == 0 and half == 0:
                                    wait_apart(pe, passed, multiplied, i * U + U)
                                m = pe.transpose(ps_turn[:, half, (k % HALF) * P:(k % HALF + 1) * P], rows[:, k, :], K.ident[:, :])
                        if xt is not None:
                            m.then_inc(turned, 1)
                            pe.wait_ge(copied, i * 2 + (half + 1))
                            for k in range(half * HALF, (half + 1) * HALF):
                                pe.matmul(ps_dot[:, half, (k % HALF) * P:(k % HALF + 1) * P], rows_t[:, k, :], xt[:, bass.ds(blocks[k] * P, P)],
                                          start=True, stop=True).then_inc(dotted, 1)
                        for k in range(half * HALF, (half + 1) * HALF):
                            pe.wait_ge(built, i * U + (k + 1))
                            pe.wait_ge(added, i * U + 1)
                            pe.matmul(part(k), hot[:, k, :], rows[:, k, :], start=True, stop=True).then_inc(multiplied, 1)


def project_sums(nc, K, total, w_fc):
    with Stage(nc, "fc") as s:
        w = s.sb("w", [D, D])
        turned = s.sb("turned", [D, 2, P])
        ps_w = s.ps("ps_w", [D, 512])
        ps_turn = s.ps("ps_turn", [D, 2, 512])
        ps_out = s.ps("ps_out", [P, 2, 512])
        wt = s.sb("wt", [D, D])
        held = s.sb("held", [P, 2, D])
        loaded, staged, flipped, copied, projected, added = [s.sem(n) for n in ("loaded", "staged", "flipped", "copied", "projected", "added")]
        passed = s.sem("passed")
        with nc.Block() as block:
            @block.sync
            def _(sp):
                sp.dma_start(w[:, :], w_fc).then_inc(loaded, 16)

            @block.gpsimd
            def _(pool):
                with pool.Fori(0, NB // 2) as i:
                    for k in range(2):
                        pool.wait_ge(flipped, i * 2 + (k + 2))
                        pool.tensor_copy(held[:, k, :], total[:, bass.ds(i * 2 + k, 1), :].rearrange("p o d -> p (o d)")).then_inc(staged, 1)

            @block.tensor
            def _(pe):
                pe.sem_inc(projected, 2)
                pe.sem_inc(flipped, 2)
                pe.wait_ge(loaded, 16)
                pe.transpose(ps_w[:, 0:D], w[:, :], K.ident[0:D, 0:D]).then_inc(flipped, 1)
                pe.wait_ge(copied, 3)
                with pe.Fori(0, NB // 2) as i:
                    for k in range(2):
                        wait_apart(pe, passed, copied, i * 2 + (k + 2))
                        wait_apart(pe, passed, staged, i * 2 + (k + 1))
                        pe.transpose(ps_turn[:, k, 0:P], held[:, k, :], K.ident[:, :]).then_inc(flipped, 1)
                    for k in range(2):
                        pe.wait_ge(copied, i * 2 + (k + 4))
                        pe.wait_ge(added, i * 2 + (k + 1))
                        pe.matmul(ps_out[:, k, 0:D], turned[:, k, :], wt[:, :], start=True, stop=True).then_inc(projected, 1)

            @block.scalar
            def _(act):
                act.sem_inc(copied, 2)
                act.wait_ge(flipped, 3)
                act.copy(wt[:, :], ps_w[:, 0:D]).then_inc(copied, 1)
                with act.Fori(0, NB // 2) as i:
                    for k in range(2):
                        act.wait_ge(flipped, i * 2 + (k + 4))
                        act.wait_ge(projected, i * 2 + (k + 1))
                        act.copy(turned[:, k, :], ps_turn[:, k, 0:P]).then_inc(copied, 1)

            @block.vector
            def _(v):
                v.sem_inc(added, 2)
                with v.Fori(0, NB // 2) as i:
                    for k in range(2):
                        v.wait_ge(projected, i * 2 + (k + 3))
                        xb = K.x[:, bass.ds(i * 2 + k, 1), :].rearrange("p o d -> p (o d)")
                        v.tensor_tensor(xb, xb, ps_out[:, k, 0:D], ALU.add).then_inc(added, 1)


def store(nc, K, out):
    with Stage(nc, "store") as s:
        stored = s.sem("stored")
        with nc.Block() as block:
            @block.sync
            def _(sp):
                sp.dma_start(out[0:FULLN * P, :].rearrange("(b p) d -> p b d", p=P), K.x[:, 0:FULLN, :]).then_inc(stored, 16)
                sp.dma_start(out[FULLN * P:N, :], K.x[0:RESTN, FULLN, :]).then_inc(stored, 16)
                sp.wait_ge(stored, 32)


class Names:
    pass


def program(nc, x, src, dst, edge_attr, etype, weight, w_lin, b_lin, w_edge, b_edge, att, bias, w_rel, w_fc, out, upto=99, dump=None):
    dump = dump or {}

    def dram(name, shape, dt=F32):
        return dump[name] if name in dump else nc.dram_tensor(name, shape, dt).ap()

    K, T, M = Names(), Names(), Names()
    M.src, M.dst, M.relrow, M.weight = [dram(n, (EP,)) for n in ("m_src", "m_dst", "m_relrow", "m_weight")]
    T.nodes = dram("t_nodes", (NP, D + HEADS))
    T.sorted = dram("t_sorted", (EP, ROWP))
    with ExitStack() as Stage.whole, Stage(nc, "k") as k:
        K.ones, K.iota, K.below, K.above, K.ident = [k.sb(n, [P, P]) for n in ("ones", "iota", "below", "above", "ident")]
        K.iota_b, K.ident_b, K.ident_128 = [k.sb(n, [P, P], BF16) for n in ("iota_b", "ident_b", "ident_128")]
        K.pcol = k.sb("pcol", [P, 1])
        K.visit_i, K.visit = k.sb("visit_i", [P, GV], I32), k.sb("visit", [P, GV])
        K.edges_i, K.edges = k.sb("edges_i", [P, NB], I32), k.sb("edges", [P, NB])
        K.x = k.sb("x", [P, NB, D])
        K.w_att = k.sb("w_att", [ROW, HEADS * D])
        K.bias = k.sb("bias", [P, D])
        constants(nc, K)
        with Stage(nc, "a") as a:
            A, G = Names(), Names()
            A.src_i, A.dst_i = a.sb("src_i", [P, NT], I32), a.sb("dst_i", [P, NT + U], I32)
            A.src_f = a.sb("src_f", [P, NT])
            load_edges(nc, K, A, src, dst, etype, weight, x, M)
            G.part = a.sb("part", [P, NT, HEADS])
            G.tail = a.sb("tail", [P, NT, ROW - C_KEY])
            A.s_node = a.sb("s_node", [P, HEADS, NB])
            attention_vectors(nc, K, A, G, w_lin, b_lin, w_edge, b_edge, att, bias, edge_attr, T)
            A.lo_f, A.hi_f = a.sb("lo_f", [P, NT]), a.sb("hi_f", [P, NT])
            A.lo, A.hi = a.sb("lo", [P, NT], BF16), a.sb("hi", [P, NT], BF16)
            A.first = a.sb("first", [P, NB])
            A.key_i = A.src_i
            with Stage(nc, "split") as s:
                split_keys(nc, A, s)
            count_places(nc, K, A, "count")
            if upto < 2:
                return
            sort_attention(nc, K, A, G, T)
        if upto < 3:
            return
        M.key, M.e = dram("m_key", (EP,)), [dram(f"m_e{h}", (EP,)) for h in range(HEADS)]
        softmax_weights(nc, K, T, M)
        if upto < 4:
            return
        T.blk, T.tile = dram("t_blk", (NVP,), I32), dram("t_tile", (NVP,), I32)
        T.blank = dram("t_blank", (2, P))
        T.rel = dram("t_rel", (NP, RELS * D))
        with Stage(nc, "v1") as a:
            V = Names()
            V.block_row, V.tile_row = a.sb("block_row", [1, NVP], I32), a.sb("tile_row", [1, NVP], I32)
            V.rel, V.e = a.sb("rel", [P, NVP]), [a.sb(f"e{h}", [P, NVP]) for h in range(HEADS)]
            make_visits(nc, K, T, "mv1", M.key, V.block_row, V.tile_row, V.rel, list(zip(M.e, V.e)))
            total = a.sb("total", [P, NB + 1, HEADS, ROW])
            sum_attention(nc, K, T, V, total)
            finish_attention(nc, K, total)
            layer_norm(nc, K, "ln0")
        if upto < 5:
            store(nc, K, out)
            return
        with Stage(nc, "v2") as a:
            V = Names()
            V.block_row, V.tile_row = a.sb("block_row", [1, NVP], I32), a.sb("tile_row", [1, NVP], I32)
            V.rel, V.weight, V.src, V.relrow = [a.sb(n, [P, NVP]) for n in ("rel", "weight", "src", "relrow")]
            make_visits(nc, K, T, "mv2", M.dst, V.block_row, V.tile_row, V.rel,
                        [(M.weight, V.weight), (M.src, V.src), (M.relrow, V.relrow)])
            total = a.sb("total", [P, NB + 1, D])
            relation_table(nc, K, T, w_rel)
            sum_rows(nc, K, V, "sum1", T.rel.rearrange("n (r d) -> (n r) d", d=D), V.relrow, total)
            layer_norm(nc, K, "ln1", total[:, 0:NB, :])
            if upto < 6:
                store(nc, K, out)
                return
            T.x2, T.x3 = dram("t_x2", (NP, D)), dram("t_x3", (NP, D))
            node_table(nc, K, "nt2", T.x2)
            sum_rows(nc, K, V, "sum2", T.x2, V.src, total, weight=V.weight)
            layer_norm(nc, K, "ln2", total[:, 0:NB, :])
            if upto < 7:
                store(nc, K, out)
                return
            with Stage(nc, "v3") as b:
                xt = b.sb("xt", [D, NP + P])
                node_table(nc, K, "nt3", T.x3)
                turn_nodes(nc, K, xt)
                sum_rows(nc, K, V, "sum3", T.x3, V.src, total, xt=xt)
            project_sums(nc, K, total, w_fc)
            layer_norm(nc, K, "ln3")
        store(nc, K, out)


_INS = ["x", "src", "dst", "edge_attr_5", "edge_type_16", "edge_weight", "L0_gnn_W_lin", "L0_gnn_b_lin", "L0_gnn_W_edge",
        "L0_gnn_b_edge", "L0_gnn_att", "L0_gnn_bias", "L1_gnn_weight", "L3_gnn_fc_weight"]


def kernel(**inputs):
    import numpy as _np
    import concourse.bacc as _bacc
    from concourse import mybir as _mybir
    from concourse.bass_utils import run_bass_kernel_spmd as _run

    nc = _bacc.Bacc("TRN2", target_bir_lowering=False, num_devices=1)
    arrays, args = {}, []
    for name in _INS:
        a = _np.ascontiguousarray(inputs[name])
        arrays[f"in_{name}_dram"] = a
        args.append(nc.dram_tensor(f"in_{name}_dram", a.shape, _mybir.dt.from_np(a.dtype), kind="ExternalInput").ap())
    out = nc.dram_tensor("out_0_dram", (N, D), _mybir.dt.float32, kind="ExternalOutput").ap()
    program(nc, *args, out)
    r = _run(nc, [arrays], core_ids=[0])
    return r.results[0]["out_0_dram"]
```

```python
from contextlib import ExitStack

import concourse.bass as bass
from concourse import mybir

P = 128
N = 12500
E = 212500
D = 64
HEADS = 2
BOND = 5
RELS = 16
NEG_SLOPE = 0.2
EPS = 1e-5
U = 16
GROUP = 4
NG = U // GROUP
NB = -(-N // P)
NP = NB * P
NT = -(-E // (P * U)) * U
EP = NT * P
LASTC = E - (P - 1) * NT
FULLN = N // P
RESTN = N - FULLN * P
PADNODE = NP - 1
VISITS = NT + NB - 1
NV = -(-VISITS // U) * U
GT = NT // P
GV = -(-NV // P)
NVP = GV * P
assert NT % P == 0 and PADNODE >= N and 0 < LASTC < NT

C_Z = D
C_KEY = C_Z + HEADS
C_ATTR = C_KEY + 1
C_ONE = C_ATTR + BOND
ROW = C_ONE + 1
ROWP = 76
LOW = -3.0e38

F32 = mybir.dt.float32
BF16 = mybir.dt.bfloat16
I32 = mybir.dt.int32
ALU = mybir.AluOpType
ACT = mybir.ActivationFunctionType
X_AXIS = mybir.AxisListType.X


class Chain:

    def __init__(self, eng, sem):
        self.eng, self.sem, self.n = eng, sem, 0

    def add(self, ins):
        self.n += 1
        return ins.then_inc(self.sem, 1)

    def link(self, ins):
        self.add(ins)
        self.eng.wait_ge(self.sem, self.n)


class Names:
    pass


class Stage:

    def __init__(self, nc, name):
        self.nc, self.name, self.ctx, self.sems = nc, name, ExitStack(), []

    whole = None

    def __enter__(self):
        return self

    def __exit__(self, *a):
        for sem in self.sems:
            self.nc.gpsimd.sem_clear(sem)
        return self.ctx.__exit__(*a)

    def sb(self, name, shape, dt=F32):
        return self.ctx.enter_context(self.nc.sbuf_tensor(f"{self.name}_{name}", shape, dt))

    def ps(self, name, shape, dt=F32):
        return self.ctx.enter_context(self.nc.psum_tensor(f"{self.name}_{name}", shape, dt))

    def sem(self, name):
        self.sems.append(self.ctx.enter_context(self.nc.semaphore(f"{self.name}_{name}")))
        return self.sems[-1]

    def pool_dma_sem(self, name):
        return Stage.whole.enter_context(self.nc.semaphore(f"{self.name}_{name}"))


def wait_apart(eng, passed, sem, value):
    eng.wait_ge(sem, value)
    eng.sem_inc(passed, 1)


def at(c):
    return bass.ds(c, 1)


def load_registers(nc, engine, row, i, high, why):
    _, values = nc.values_load_multi_w_load_instructions(
        row[0:1, bass.ds(i * U, U)], engines=[engine], min_val=0, max_val=high,
        skip_runtime_bounds_check_because=why)
    return values


def constants(nc, K):
    with Stage(nc, "const") as s:
        ints = s.sb("ints", [P, P + 1], I32)
        made, chain = s.sem("made"), s.sem("chain")
        with nc.Block() as block:
            @block.gpsimd
            def _(pool):
                pool.iota(ints[:, 0:P], [[1, P]], base=0, channel_multiplier=0)
                pool.iota(ints[:, P:P + 1], [[0, 1]], base=0, channel_multiplier=1)
                pool.iota(K.visit_i[:, :], [[P, GV]], base=0, channel_multiplier=1)
                pool.iota(K.edges_i[:, :], [[P, NB]], base=P, channel_multiplier=0).then_inc(made, 1)

            @block.vector
            def _(v):
                c = Chain(v, chain)
                v.wait_ge(made, 1)
                v.memset(K.ones[:, :], 1.0)
                v.tensor_copy(K.visit[:, :], K.visit_i[:, :])
                v.tensor_copy(K.edges[:, :], K.edges_i[:, :])
                v.tensor_copy(K.pcol[:, :], ints[:, P:P + 1])
                c.link(v.tensor_copy(K.iota[:, :], ints[:, 0:P]))
                v.tensor_copy(K.iota_b[:, :], K.iota[:, :])
                v.tensor_scalar(K.below[:, :], K.iota[:, :], K.pcol[:, 0:1], None, ALU.is_lt)
                v.tensor_scalar(K.above[:, :], K.iota[:, :], K.pcol[:, 0:1], None, ALU.is_gt)
                c.link(v.tensor_scalar(K.ident[:, :], K.iota[:, :], K.pcol[:, 0:1], None, ALU.is_equal))
                v.tensor_copy(K.ident_b[:, :], K.ident[:, :])
                v.tensor_scalar(K.ident_128[:, :], K.ident[:, :], float(P), None, ALU.mult)


def load_edges(nc, K, A, src, dst, etype, weight, x, M):
    with Stage(nc, "edges") as s:
        typ = s.sb("typ", [P, NT], I32)
        w = s.sb("w", [P, NT])
        a1 = s.sb("a1", [P, NT])
        d1 = s.sb("d1", [P, NT])
        padded, loaded, ready, stored, chain = s.sem("padded"), s.sem("loaded"), s.sem("ready"), s.sem("stored"), s.sem("chain")
        with nc.Block() as block:
            @block.sync
            def _(sp):
                sp.wait_ge(padded, 1)
                for where, what in ((A.src_i, src), (A.dst_i, dst), (typ, etype), (w, weight)):
                    sp.dma_start(where[0:P - 1, 0:NT], what[0:(P - 1) * NT].rearrange("(p c) -> p c", c=NT)).then_inc(loaded, 16)
                    sp.dma_start(where[P - 1:P, 0:LASTC], what[(P - 1) * NT:E].rearrange("(p c) -> p c", p=1)).then_inc(loaded, 16)
                sp.dma_start(K.x[:, 0:FULLN, :], x[0:FULLN * P, :].rearrange("(b p) d -> p b d", p=P)).then_inc(loaded, 16)
                sp.dma_start(K.x[0:RESTN, FULLN, :], x[FULLN * P:N, :]).then_inc(loaded, 16)
                sp.wait_ge(ready, 1)
                sp.dma_start(M.src.rearrange("(p c) -> p c", c=NT), A.src_f[:, :]).then_inc(stored, 16)
                sp.dma_start(M.dst.rearrange("(p c) -> p c", c=NT), d1[:, :]).then_inc(stored, 16)
                sp.dma_start(M.relrow.rearrange("(p c) -> p c", c=NT), a1[:, :]).then_inc(stored, 16)
                sp.dma_start(M.weight.rearrange("(p c) -> p c", c=NT), w[:, :]).then_inc(stored, 16)
                sp.wait_ge(stored, 64)

            @block.vector
            def _(v):
                c = Chain(v, chain)
                v.memset(A.src_i[:, :], PADNODE)
                v.memset(A.dst_i[:, :], PADNODE)
                v.memset(typ[:, :], 0)
                v.memset(w[:, :], 0.0)
                c.link(v.memset(K.x[:, :, :], 0.0))
                v.sem_inc(padded, 1)
                v.wait_ge(loaded, 160)
                v.tensor_copy(A.src_f[:, :], A.src_i[:, :])
                v.tensor_copy(d1[:, :], A.dst_i[:, 0:NT])
                c.link(v.tensor_copy(a1[:, :], typ[:, :]))
                v.scalar_tensor_tensor(a1[:, :], A.src_f[:, :], float(RELS), a1[:, :], ALU.mult, ALU.add).then_inc(ready, 1)


def split_keys(nc, A, s):
    tmp_lo, tmp_hi, chain = s.sb("tmp_lo", [P, NT], I32), s.sb("tmp_hi", [P, NT], I32), s.sem("split_chain")
    with nc.Block() as block:
        @block.vector
        def _(v):
            c = Chain(v, chain)
            v.tensor_scalar(tmp_lo[:, :], A.key_i[:, :], P - 1, None, ALU.bitwise_and)
            c.link(v.tensor_scalar(tmp_hi[:, :], A.key_i[:, :], 7, None, ALU.logical_shift_right))
            v.tensor_copy(A.lo_f[:, :], tmp_lo[:, :])
            v.tensor_copy(A.hi_f[:, :], tmp_hi[:, :])
            v.tensor_copy(A.lo[:, :], tmp_lo[:, :])
            c.link(v.tensor_copy(A.hi[:, :], tmp_hi[:, :]))


def count_places(nc, K, A, name):
    with Stage(nc, name) as s:
        onehot_lo = s.sb("onehot_lo", [P, U, P], BF16)
        onehot_hi = s.sb("onehot_hi", [P, U, NB], BF16)
        counts = s.sb("counts", [P, NB])
        totals = s.sb("totals", [P, NB])
        upto = s.sb("upto", [P, NB])
        zeros = s.sb("zeros", [P, NB])
        zeros_b = s.sb("zeros_b", [P, P], BF16)
        ps_count = s.ps("ps_count", [P, 512])
        ps_sums = s.ps("ps_sums", [P, 512])
        chain, hot, used, copied, summed = [s.sem(n) for n in ("chain", "hot", "used", "copied", "summed")]
        with nc.Block() as block:
            @block.vector
            def _(v):
                c = Chain(v, chain)
                v.memset(zeros[:, :], 0.0)
                v.memset(zeros_b[:, :], 0.0).then_inc(hot, 1)
                with v.Fori(0, NT // U) as i:
                    v.wait_ge(used, i + 1)
                    for k in range(U):
                        v.tensor_scalar(onehot_lo[:, k, :], K.iota_b[:, :], A.lo_f[:, at(i * U + k)], None, ALU.is_equal)
                        v.tensor_scalar(onehot_hi[:, k, :], K.iota_b[:, 0:NB], A.hi_f[:, at(i * U + k)], None,
                                        ALU.is_equal).then_inc(hot, 1)
                v.wait_ge(used, NT // U + 1)
                v.tensor_copy(counts[:, :], ps_count[:, 0:NB]).then_inc(copied, 1)
                v.wait_ge(summed, 1)
                c.link(v.tensor_copy(totals[:, :], ps_sums[:, P:P + NB]))
                c.link(v.tensor_tensor_scan(upto[:, :], totals[:, :], zeros[:, :], 0.0, ALU.add, ALU.add))
                c.link(v.tensor_tensor(upto[:, :], upto[:, :], totals[:, :], ALU.subtract))
                c.link(v.tensor_tensor(A.first[:, :], upto[:, :], ps_sums[:, 0:NB], ALU.add))

            @block.tensor
            def _(pe):
                pe.wait_ge(hot, 1)
                pe.matmul(ps_count[:, 0:NB], zeros_b[:, :], zeros_b[:, 0:NB], start=True, stop=True).then_inc(used, 1)
                with pe.Fori(0, NT // U) as i:
                    for k in range(U):
                        pe.wait_ge(hot, i * U + (k + 2))
                        m = pe.matmul(ps_count[:, 0:NB], onehot_lo[:, k, :], onehot_hi[:, k, :], start=False, stop=True,
                                      skip_group_check=True)
                    m.then_inc(used, 1)
                pe.wait_ge(copied, 1)
                pe.matmul(ps_sums[:, 0:NB], K.above[:, :], counts[:, :], start=True, stop=True)
                pe.matmul(ps_sums[:, P:P + NB], K.ones[:, :], counts[:, :], start=True, stop=True).then_inc(summed, 1)


def attention_vectors(nc, K, A, G, w_lin, b_lin, w_edge, b_edge, att, bias, edge_attr, T):
    with Stage(nc, "vectors") as s:
        side = s.sb("side", [D, HEADS, D + BOND + 2])
        att_c = s.sb("att_c", [D, HEADS, 2])
        att_b = s.sb("att_b", [D, HEADS, 2, P])
        vec = s.sb("vec", [P, HEADS, 2, D + BOND + 2])
        prod = s.sb("prod", [P, NB, D])
        node_z = s.sb("node_z", [P, NB, HEADS])
        attr = s.sb("attr", [P, NT, BOND])
        wb = s.sb("wb", [ROW, HEADS * D])
        const = s.sb("const", [P, HEADS])
        ps_vec = s.ps("ps_vec", [P, 512])
        loaded, chain, spread, multiplied, stored, padded = [s.sem(n) for n in ("loaded", "chain", "spread", "multiplied", "stored", "padded")]
        NL = 16 * (2 * HEADS + 2 + HEADS + 2 + 5 + 1)
        with nc.Block() as block:
            @block.sync
            def _(sp):
                sp.wait_ge(padded, 1)
                with nc.allow_non_contiguous_dma(reason="small transposed weights"):
                    for h in range(HEADS):
                        cols = slice(h * D, (h + 1) * D)
                        sp.dma_start(side[:, h, 0:D], w_lin[:, cols].rearrange("k d -> d k")).then_inc(loaded, 16)
                        sp.dma_start(side[:, h, D:D + BOND], w_edge[:, cols].rearrange("k d -> d k")).then_inc(loaded, 16)
                        sp.dma_start(att_c[:, h, :], att[0, h, :].rearrange("(s d) -> d s", s=2)).then_inc(loaded, 16)
                    sp.dma_start(side[:, :, D + BOND:D + BOND + 1], b_lin.rearrange("(h d o) -> d h o", d=D, o=1)).then_inc(loaded, 16)
                    sp.dma_start(side[:, :, D + BOND + 1:D + BOND + 2], b_edge.rearrange("(h d o) -> d h o", d=D, o=1)).then_inc(loaded, 16)
                sp.dma_start(attr[0:P - 1, :, :], edge_attr[0:(P - 1) * NT, :].rearrange("(p c) k -> p c k", c=NT)).then_inc(loaded, 16)
                sp.dma_start(attr[P - 1:P, 0:LASTC, :], edge_attr[(P - 1) * NT:E, :].rearrange("(p c) k -> p c k", p=1)).then_inc(loaded, 16)
                sp.dma_start(K.w_att[0:D, :], w_lin).then_inc(loaded, 16)
                sp.dma_start(K.w_att[C_ATTR:C_ONE, :], w_edge).then_inc(loaded, 16)
                sp.dma_start(K.w_att[C_ONE:ROW, :], b_lin.rearrange("(a n) -> a n", a=1)).then_inc(loaded, 16)
                sp.dma_start(wb[C_ONE:ROW, :], b_edge.rearrange("(a n) -> a n", a=1)).then_inc(loaded, 16)
                sp.dma_start(K.bias[:, :], bias.rearrange("(a n) -> a n", a=1).to_broadcast([P, D])).then_inc(loaded, 16)
                sp.dma_start(T.nodes[:, 0:D].rearrange("(b p) d -> p b d", p=P), K.x[:, :, :]).then_inc(loaded, 16)
                sp.wait_ge(stored, 1)
                sp.dma_start(T.nodes[:, D:D + HEADS].rearrange("(b p) d -> p b d", p=P), node_z[:, :, :]).then_inc(loaded, 16)
                sp.wait_ge(loaded, NL + 16)

            @block.vector
            def _(v):
                c = Chain(v, chain)
                v.memset(attr[:, :, :], 0.0)
                v.memset(K.w_att[:, :], 0.0)
                c.link(v.memset(wb[:, :], 0.0))
                v.sem_inc(padded, 1)
                v.wait_ge(loaded, NL)
                c.link(v.tensor_tensor(K.w_att[:, :], K.w_att[:, :], wb[:, :], ALU.add))
                for h in range(HEADS):
                    for e in range(2):
                        last = v.tensor_scalar(att_b[:, h, e, :], K.ones[0:D, :], att_c[:, h, e:e + 1], None, ALU.mult)
                last.then_inc(spread, 1)
                v.wait_ge(multiplied, 1)
                c.link(v.tensor_copy(vec[:, :, :, :], ps_vec[:, 0:HEADS * 2 * (D + BOND + 2)].rearrange("p (h e n) -> p h e n", h=HEADS, e=2)))
                bl, be = D + BOND, D + BOND + 1
                c.link(v.tensor_tensor(const[:, :], vec[:, :, 0, bl], vec[:, :, 1, bl], ALU.add))
                c.link(v.tensor_tensor(const[:, :], const[:, :], vec[:, :, 1, be], ALU.add))
                for h in range(HEADS):
                    for e in range(2):
                        c.link(v.tensor_tensor(prod[:, :, :], K.x[:, :, :], vec[:, h, e:e + 1, 0:D].to_broadcast([P, NB, D]), ALU.mult))
                        if e == 0:
                            c.link(v.tensor_reduce(A.s_node[:, h, :], prod[:, :, :], X_AXIS, ALU.add))
                            c.link(v.tensor_scalar(A.s_node[:, h, :], A.s_node[:, h, :], const[:, h:h + 1], None, ALU.add))
                        else:
                            c.link(v.tensor_reduce(node_z[:, :, h], prod[:, :, :], X_AXIS, ALU.add))
                v.sem_inc(stored, 1)
                for h in range(HEADS):
                    c.link(v.tensor_scalar(G.part[:, :, h], attr[:, :, 0], vec[:, h, 1, D:D + 1], None, ALU.mult))
                    for k in range(1, BOND):
                        c.link(v.scalar_tensor_tensor(G.part[:, :, h], attr[:, :, k], vec[:, h, 1, D + k:D + k + 1], G.part[:, :, h],
                                                      ALU.mult, ALU.add))
                v.tensor_copy(G.tail[:, :, 0], A.src_f[:, :])
                v.tensor_copy(G.tail[:, :, 1:1 + BOND], attr[:, :, :])
                v.memset(G.tail[:, :, 1 + BOND], 1.0)

            @block.tensor
            def _(pe):
                pe.wait_ge(spread, 1)
                n = D + BOND + 2
                for h in range(HEADS):
                    for e in range(2):
                        o = (2 * h + e) * n
                        m = pe.matmul(ps_vec[:, o:o + n], att_b[:, h, e, :], side[:, h, :], start=True, stop=True)
                m.then_inc(multiplied, 1)


def sort_attention(nc, K, A, G, T):
    with Stage(nc, "sort") as s:
        hot_lo = s.sb("hot_lo", [P, U, P], BF16)
        hot_hi = s.sb("hot_hi", [P, U, NB], BF16)
        looked_up = s.sb("looked_up", [P, 2, P])
        places = s.sb("places", [P, 2, NB])
        junk_a = s.sb("junk_a", [P, U, P])
        junk_b = s.sb("junk_b", [P, U, 3, NB])
        rank = s.sb("rank", [P, U])
        found = s.sb("found", [P, 3, U])
        z = s.sb("z", [P, U, HEADS])
        pos = s.sb("pos", [P, U], I32)
        fetch = s.sb("fetch", [P, U], I32)
        rec = s.sb("rec", [P, U, ROWP])
        blank = s.sb("blank", [P, ROWP])
        ps_same = s.ps("ps_same", [P, 2, 512])
        ps_hot = s.ps("ps_hot", [P, 2, 1024], BF16)
        ps_find = s.ps("ps_find", [P, 2, 512])
        ps_place = s.ps("ps_place", [P, 512])
        names = ("chain", "hot", "same", "ranked", "turned", "turn_copied", "found_ready", "found_used", "updated",
                 "place_copied", "tail_ready", "rec_ready", "cleared", "fetch_ready")
        (chain, hot, same, ranked, turned, turn_copied, found_ready, found_used, updated,
         place_copied, tail_ready, rec_ready, cleared, fetch_ready) = [s.sem(n) for n in names]
        got = [s.pool_dma_sem(f"got{k}") for k in range(U)]
        sent = [s.pool_dma_sem(f"sent{k}") for k in range(U)]
        passed = s.sem("passed")
        with nc.Block() as block:
            @block.gpsimd
            def _(pool):
                pool.wait_ge(cleared, 1)
                for k in range(U):
                    pool.dma_start(rec[:, k, :], blank[:, :]).then_inc(sent[k], 16)
                with pool.Fori(0, NT // U) as i:
                    for k in range(U):
                        wait_apart(pool, passed, sent[k], i * 16 + 16)
                        if k % GROUP == 0:
                            wait_apart(pool, passed, fetch_ready, i * NG + (k // GROUP + 1))
                        pool.indirect_dma_start(rec[:, k, 0:D + HEADS], None, T.nodes,
                                                bass.IndirectOffsetOnAxis(fetch[:, k:k + 1], axis=0)).then_inc(got[k], 16)
                    for g in range(NG):
                        wait_apart(pool, passed, tail_ready, i * NG + (g + 1))
                        wait_apart(pool, passed, rec_ready, i * NG + (g + 1))
                        for k in range(g * GROUP, (g + 1) * GROUP):
                            pool.indirect_dma_start(T.sorted, bass.IndirectOffsetOnAxis(pos[:, k:k + 1], axis=0),
                                                    rec[:, k, :], None).then_inc(sent[k], 16)
                for k in range(U):
                    pool.wait_ge(sent[k], 16 * (NT // U + 1))

            @block.vector
            def _(v):
                c = Chain(v, chain)
                v.memset(blank[:, :], 0.0).then_inc(cleared, 1)
                v.sem_inc(ranked, 2)
                v.sem_inc(found_used, 2)
                with v.Fori(0, NT // U) as i:
                    t0 = i * U
                    v.wait_ge(found_used, t0 + 2)
                    for k in range(U):
                        v.wait_ge(updated, t0 + (k + 1))
                        v.tensor_scalar(hot_lo[:, k, :], K.iota_b[:, :], A.lo_f[:, at(t0 + k)], None, ALU.is_equal)
                        v.tensor_scalar(hot_hi[:, k, :], K.iota_b[:, 0:NB], A.hi_f[:, at(t0 + k)], None,
                                        ALU.is_equal).then_inc(hot, 1)
                    v.wait_ge(hot, t0 + U)
                    for g in range(NG):
                        ks = slice(g * GROUP, (g + 1) * GROUP)
                        for k in range(g * GROUP, (g + 1) * GROUP):
                            v.wait_ge(same, t0 + (k + 1))
                            v.scalar_tensor_tensor(junk_a[:, k, :], ps_same[:, k % 2, 0:P], A.src_f[:, at(t0 + k)], K.below[:, :],
                                                   ALU.is_equal, ALU.mult, accum_out=rank[:, k:k + 1]).then_inc(ranked, 1)
                            v.wait_ge(found_ready, t0 + (k + 3))
                            for j in range(3):
                                m = v.scalar_tensor_tensor(junk_b[:, k, j, :], ps_find[:, k % 2, j * NB:(j + 1) * NB], 1.0,
                                                           hot_hi[:, k, :], ALU.mult, ALU.mult, accum_out=found[:, j, k:k + 1])
                            m.then_inc(found_used, 1)
                        v.wait_ge(found_used, t0 + ((g + 1) * GROUP + 2))
                        for k in range(g * GROUP, (g + 1) * GROUP):
                            v.wait_ge(sent[k], i * 16 + 16)
                        v.tensor_tensor(pos[:, ks], found[:, 0, ks], rank[:, ks], ALU.add)
                        v.tensor_tensor(z[:, ks, :], found[:, 1:3, ks].rearrange("p h k -> p k h"),
                                        G.part[:, bass.ds(t0 + g * GROUP, GROUP), :], ALU.add).then_inc(chain, 1)
                        v.wait_ge(chain, i * NG + (g + 1))
                        for k in range(g * GROUP, (g + 1) * GROUP):
                            v.wait_ge(got[k], i * 16 + 16)
                        v.tensor_tensor(rec[:, ks, C_Z:C_KEY], rec[:, ks, C_Z:C_KEY], z[:, ks, :], ALU.add).then_inc(rec_ready, 1)

            @block.scalar
            def _(act):
                act.copy(places[:, 0, :], A.first[:, :]).then_inc(place_copied, 1)
                act.sem_inc(turn_copied, 2)
                for g in range(NG):
                    ks = slice(g * GROUP, (g + 1) * GROUP)
                    act.copy(fetch[:, ks], A.dst_i[:, ks]).then_inc(fetch_ready, 1)
                with act.Fori(0, NT // U) as i:
                    t0 = i * U
                    for g in range(NG):
                        ks = slice(g * GROUP, (g + 1) * GROUP)
                        for k in range(g * GROUP, (g + 1) * GROUP):
                            act.wait_ge(sent[k], i * 16 + 16)
                        act.copy(rec[:, ks, C_KEY:ROW], G.tail[:, bass.ds(t0 + g * GROUP, GROUP), :]).then_inc(tail_ready, 1)
                        for k in range(g * GROUP, (g + 1) * GROUP):
                            act.wait_ge(turned, t0 + (k + 1))
                            act.wait_ge(found_ready, t0 + (k + 1))
                            act.copy(looked_up[:, k % 2, :], ps_hot[:, k % 2, 0:P]).then_inc(turn_copied, 1)
                            act.wait_ge(updated, t0 + (U + k + 1))
                            act.wait_ge(found_ready, t0 + (k + 2))
                            act.copy(places[:, (k + 1) % 2, :], ps_place[:, 0:NB]).then_inc(place_copied, 1)
                        for k in range(g * GROUP, (g + 1) * GROUP):
                            act.wait_ge(got[k], i * 16 + 16)
                        act.copy(fetch[:, ks], A.dst_i[:, bass.ds(t0 + (U + g * GROUP), GROUP)]).then_inc(fetch_ready, 1)

            @block.tensor
            def _(pe):
                pe.sem_inc(found_ready, 2)
                pe.matmul(ps_place[:, 0:NB], K.ident[:, :], A.first[:, :], start=True, stop=True).then_inc(updated, U)
                with pe.Fori(0, NT // U) as i:
                    t0 = i * U
                    for k in range(U):
                        pe.wait_ge(hot, t0 + (k + 1))
                        pe.wait_ge(ranked, t0 + (k + 1))
                        pe.matmul(ps_same[:, k % 2, 0:P], A.hi[:, at(t0 + k)].to_broadcast([P, P]), K.ident_128[:, :],
                                  start=True, stop=False)
                        pe.matmul(ps_same[:, k % 2, 0:P], A.lo[:, at(t0 + k)].to_broadcast([P, P]), K.ident_b[:, :],
                                  start=False, stop=True).then_inc(same, 1)
                        pe.wait_ge(turn_copied, t0 + (k + 1))
                        pe.transpose(ps_hot[:, k % 2, 0:P], hot_lo[:, k, :], K.ident_b[:, :]).then_inc(turned, 1)
                        pe.wait_ge(place_copied, t0 + (k + 1))
                        pe.matmul(ps_place[:, 0:NB], hot_lo[:, k, :], hot_hi[:, k, :], start=False, stop=True,
                                  skip_group_check=True).then_inc(updated, 1)
                        pe.wait_ge(turn_copied, t0 + (k + 3))
                        pe.wait_ge(found_used, t0 + (k + 1))
                        pe.matmul(ps_find[:, k % 2, 0:NB], looked_up[:, k % 2, :], places[:, k % 2, :], start=True, stop=True)
                        pe.matmul(ps_find[:, k % 2, NB:3 * NB], looked_up[:, k % 2, :],
                                  A.s_node[:, :, :].rearrange("p h b -> p (h b)"), start=True, stop=True).then_inc(found_ready, 1)


def find_disorder(nc, K, M):
    with Stage(nc, "order") as s:
        now, before = s.sb("now", [P, NT]), s.sb("before", [P, NT])
        less = s.sb("less", [P, NT])
        count = s.sb("count", [P, 1])
        ps = s.ps("ps", [P, 512])
        loaded, cleared, chain, counted, summed = [s.sem(n) for n in ("loaded", "cleared", "chain", "counted", "summed")]
        with nc.Block() as block:
            @block.sync
            def _(sp):
                sp.wait_ge(cleared, 1)
                sp.dma_start(now[:, :], M.dst.rearrange("(p c) -> p c", c=NT)).then_inc(loaded, 16)
                sp.dma_start(before[1:P, :], M.dst[NT - 1:EP - 1].rearrange("(p c) -> p c", c=NT)).then_inc(loaded, 16)
                sp.dma_start(before[0:1, 1:NT], M.dst[0:NT - 1].rearrange("(p c) -> p c", p=1)).then_inc(loaded, 16)

            @block.vector
            def _(v):
                c = Chain(v, chain)
                v.memset(before[:, :], 0.0).then_inc(cleared, 1)
                v.wait_ge(loaded, 48)
                c.link(v.tensor_tensor(less[:, :], now[:, :], before[:, :], ALU.is_lt))
                v.tensor_reduce(count[:, :], less[:, :], X_AXIS, ALU.add).then_inc(counted, 1)
                v.wait_ge(summed, 1)
                v.tensor_scalar(K.disorder[:, :], ps[0:1, 0:1], 1.0, None, ALU.min)

            @block.tensor
            def _(pe):
                pe.wait_ge(counted, 1)
                pe.matmul(ps[:, 0:1], K.ones[:, :], count[:, :], start=True, stop=True).then_inc(summed, 1)


def sort_records(nc, K, A, M):
    with Stage(nc, "resort") as s:
        pay = s.sb("pay", [P, NT, 4])
        hot_lo = s.sb("hot_lo", [P, P], BF16)
        hot_hi = s.sb("hot_hi", [P, NB], BF16)
        turned_hot = s.sb("turned_hot", [P, P])
        places = s.sb("places", [P, NB])
        junk_a, junk_b = s.sb("junk_a", [P, P]), s.sb("junk_b", [P, NB])
        rank, found, pos, rec = s.sb("rank", [P, 1]), s.sb("found", [P, 1]), s.sb("pos", [P, 1], I32), s.sb("rec", [P, 4])
        ps_same, ps_find, ps_place = s.ps("ps_same", [P, 512]), s.ps("ps_find", [P, 512]), s.ps("ps_place", [P, 512])
        ps_hot = s.ps("ps_hot", [P, 1024], BF16)
        loaded, packed, hot, turned, turn_copied, looked, place_copied, ranked, placed, rec_copied, passed, cleared, unpacked = [
            s.sem(n) for n in ("loaded", "packed", "hot", "turned", "turn_copied", "looked", "place_copied", "ranked", "placed",
                               "rec_copied", "passed", "cleared", "unpacked")]
        sent = s.pool_dma_sem("sent")
        with nc.Block() as block:
            @block.sync
            def _(sp):
                with nc.allow_non_contiguous_dma(reason="four arrays become records, off the usual path"):
                    for j, a in enumerate((M.src, M.dst, M.relrow, M.weight)):
                        sp.dma_start(pay[:, :, j:j + 1], a.rearrange("(p c o) -> p c o", c=NT, o=1)).then_inc(loaded, 16)
                    sp.wait_ge(sent, 16 * (NT + 1))
                    for j, a in enumerate((M.src, M.dst, M.relrow, M.weight)):
                        sp.dma_start(a.rearrange("(p c o) -> p c o", c=NT, o=1),
                                     M.records[:, j:j + 1].rearrange("(p c) o -> p c o", c=NT)).then_inc(unpacked, 16)
                    sp.wait_ge(unpacked, 64)

            @block.vector
            def _(v):
                v.memset(rec[:, :], 0.0).then_inc(cleared, 1)
                with v.Fori(0, NT) as t:
                    v.wait_ge(sent, t * 16 + 16)
                    v.wait_ge(looked, t + 1)
                    v.tensor_scalar(hot_lo[:, :], K.iota_b[:, :], A.lo_f[:, at(t)], None, ALU.is_equal)
                    v.tensor_scalar(hot_hi[:, :], K.iota_b[:, 0:NB], A.hi_f[:, at(t)], None, ALU.is_equal).then_inc(hot, 1)
                    v.wait_ge(hot, t + 1)
                    v.wait_ge(looked, t + 2)
                    v.scalar_tensor_tensor(junk_a[:, :], ps_same[:, 0:P], A.key_f[:, at(t)], K.below[:, :], ALU.is_equal, ALU.mult,
                                           accum_out=rank[:, :])
                    v.scalar_tensor_tensor(junk_b[:, :], ps_find[:, 0:NB], 1.0, hot_hi[:, :], ALU.mult, ALU.mult,
                                           accum_out=found[:, :]).then_inc(ranked, 1)
                    v.wait_ge(ranked, t + 1)
                    v.tensor_tensor(pos[:, :], found[:, :], rank[:, :], ALU.add).then_inc(placed, 1)

            @block.scalar
            def _(act):
                act.copy(places[:, :], A.first[:, :]).then_inc(place_copied, 1)
                act.wait_ge(loaded, 64)
                with act.Fori(0, NT) as t:
                    act.wait_ge(sent, t * 16 + 16)
                    act.copy(rec[:, :], pay[:, at(t), :].rearrange("p o w -> p (o w)")).then_inc(rec_copied, 1)
                    act.wait_ge(turned, t + 1)
                    act.copy(turned_hot[:, :], ps_hot[:, 0:P]).then_inc(turn_copied, 1)
                    act.wait_ge(looked, t + 2)
                    act.copy(places[:, :], ps_place[:, 0:NB]).then_inc(place_copied, 1)

            @block.tensor
            def _(pe):
                pe.matmul(ps_place[:, 0:NB], K.ident[:, :], A.first[:, :], start=True, stop=True).then_inc(looked, 1)
                with pe.Fori(0, NT) as t:
                    pe.wait_ge(hot, t + 1)
                    pe.matmul(ps_same[:, 0:P], A.hi[:, at(t)].to_broadcast([P, P]), K.ident_128[:, :], start=True, stop=False)
                    pe.matmul(ps_same[:, 0:P], A.lo[:, at(t)].to_broadcast([P, P]), K.ident_b[:, :], start=False, stop=True)
                    pe.transpose(ps_hot[:, 0:P], hot_lo[:, :], K.ident_b[:, :]).then_inc(turned, 1)
                    pe.wait_ge(turn_copied, t + 1)
                    pe.wait_ge(place_copied, t + 1)
                    pe.matmul(ps_find[:, 0:NB], turned_hot[:, :], places[:, :], start=True, stop=True)
                    pe.matmul(ps_place[:, 0:NB], hot_lo[:, :], hot_hi[:, :], start=False, stop=True,
                              skip_group_check=True).then_inc(looked, 1)

            @block.gpsimd
            def _(pool):
                pool.wait_ge(cleared, 1)
                pool.dma_start(M.records[0:P, :], rec[:, :]).then_inc(sent, 16)
                with pool.Fori(0, NT) as t:
                    wait_apart(pool, passed, sent, t * 16 + 16)
                    wait_apart(pool, passed, rec_copied, t + 1)
                    wait_apart(pool, passed, placed, t + 1)
                    pool.indirect_dma_start(M.records, bass.IndirectOffsetOnAxis(pos[:, :], axis=0), rec[:, :], None).then_inc(sent, 16)


def order_destinations(nc, K, M):
    find_disorder(nc, K, M)
    disorder = nc.values_load(K.disorder[0:1, 0:1], min_val=0, max_val=1,
                              skip_runtime_bounds_check_because="it is the smaller of a count and 1")
    with nc.If(disorder > 0):
        nc.all_engine_barrier()
        with Stage(nc, "b") as a:
            A = Names()
            A.key_i, A.key_f = a.sb("key_i", [P, NT], I32), a.sb("key_f", [P, NT])
            A.lo_f, A.hi_f = a.sb("lo_f", [P, NT]), a.sb("hi_f", [P, NT])
            A.lo, A.hi = a.sb("lo", [P, NT], BF16), a.sb("hi", [P, NT], BF16)
            A.first = a.sb("first", [P, NB])
            with Stage(nc, "keys") as s:
                loaded = s.sem("loaded")
                with nc.Block() as block:
                    @block.sync
                    def _(sp):
                        sp.dma_start(A.key_f[:, :], M.dst.rearrange("(p c) -> p c", c=NT)).then_inc(loaded, 16)

                    @block.vector
                    def _(v):
                        v.wait_ge(loaded, 16)
                        v.tensor_copy(A.key_i[:, :], A.key_f[:, :])
            with Stage(nc, "resplit") as s:
                split_keys(nc, A, s)
            count_places(nc, K, A, "recount")
            sort_records(nc, K, A, M)


def softmax_weights(nc, K, T, M):
    with Stage(nc, "soft") as s:
        zk = s.sb("zk", [P, NT, HEADS + 1])
        key = s.sb("key", [P, NT])
        skip = s.sb("skip", [P, NT])
        skip_b = s.sb("skip_b", [P, NT])
        most = s.sb("most", [P, HEADS, NT])
        leaky = s.sb("leaky", [P, HEADS, NT])
        scratch = s.sb("scratch", [P, HEADS, NT])
        edge = s.sb("edge", [P, 6])
        row = s.sb("row", [1, 6, P])
        r = s.sb("r", [1, 8, P])
        carry_r = s.sb("carry_r", [1, 4, P])
        carry = s.sb("carry", [P, 4])
        loaded, chain, ends, turned, carried, brought, ready, raised, stored = [
            s.sem(n) for n in ("loaded", "chain", "ends", "turned", "carried", "brought", "ready", "raised", "stored")]
        with nc.Block() as block:
            @block.sync
            def _(sp):
                sp.dma_start(zk[:, :, :], T.sorted[:, C_Z:C_KEY + 1].rearrange("(p c) w -> p c w", c=NT)).then_inc(loaded, 16)
                sp.wait_ge(ends, 1)
                with nc.allow_non_contiguous_dma(reason="a column of 128 words becomes a row"):
                    for j in range(6):
                        sp.dma_start(row[0:1, j, :], edge[:, j:j + 1]).then_inc(turned, 16)
                    sp.wait_ge(carried, 1)
                    for j in range(4):
                        sp.dma_start(carry[:, j:j + 1], carry_r[0:1, j, :]).then_inc(brought, 16)
                sp.wait_ge(raised, 1)
                sp.dma_start(M.key.rearrange("(p c) -> p c", c=NT), key[:, :]).then_inc(stored, 16)
                for h in range(HEADS):
                    sp.dma_start(M.e[h].rearrange("(p c) -> p c", c=NT), scratch[:, h, :]).then_inc(stored, 16)
                sp.wait_ge(stored, 16 * (1 + HEADS))

            @block.vector
            def _(v):
                c = Chain(v, chain)
                v.wait_ge(loaded, 16)
                c.link(v.tensor_copy(key[:, :], zk[:, :, HEADS]))
                v.memset(skip[:, 0:1], LOW)
                v.memset(skip_b[:, NT - 1:NT], LOW)
                v.tensor_scalar(edge[:, 0:1], key[:, 0:1], 1.0, None, ALU.mult)
                v.tensor_scalar(edge[:, 1:2], key[:, NT - 1:NT], 1.0, None, ALU.mult)
                c.link(v.tensor_tensor(skip[:, 1:NT], key[:, 1:NT], key[:, 0:NT - 1], ALU.not_equal))
                c.link(v.tensor_scalar(skip[:, 1:NT], skip[:, 1:NT], LOW, None, ALU.mult))
                c.link(v.tensor_copy(skip_b[:, 0:NT - 1], skip[:, 1:NT]))
                for h in range(HEADS):
                    c.link(v.tensor_tensor_scan(scratch[:, h, :], skip[:, :], zk[:, :, h], 0.0, ALU.add, ALU.max))
                    c.link(v.tensor_tensor_scan(most[:, h, ::-1], skip_b[:, ::-1], scratch[:, h, ::-1], 0.0, ALU.add, ALU.max))
                    v.tensor_copy(edge[:, 2 + h:3 + h], most[:, h, 0:1])
                    c.link(v.tensor_copy(edge[:, 4 + h:5 + h], most[:, h, NT - 1:NT]))
                v.sem_inc(ends, 1)
                v.wait_ge(turned, 96)
                c.link(v.memset(r[:, :, :], LOW))
                v.tensor_tensor(r[0:1, 0, 1:P], row[0:1, 0, 1:P], row[0:1, 1, 0:P - 1], ALU.not_equal)
                c.link(v.tensor_tensor(r[0:1, 1, :], row[0:1, 0, :], row[0:1, 1, :], ALU.not_equal))
                v.tensor_scalar(r[0:1, 0, 1:P], r[0:1, 0, 1:P], LOW, None, ALU.mult)
                c.link(v.tensor_scalar(r[0:1, 1, :], r[0:1, 1, :], LOW, None, ALU.mult))
                v.tensor_tensor(r[0:1, 2, :], r[0:1, 0, :], r[0:1, 1, :], ALU.min)
                c.link(v.tensor_tensor(r[0:1, 3, 0:P - 1], r[0:1, 0, 1:P], r[0:1, 1, 0:P - 1], ALU.min))
                c.link(v.memset(carry_r[:, :, :], LOW))
                for h in range(HEADS):
                    v.tensor_tensor_scan(r[0:1, 4 + h, :], r[0:1, 2, :], row[0:1, 4 + h, :], 0.0, ALU.add, ALU.max)
                    c.link(v.tensor_tensor_scan(r[0:1, 6 + h, ::-1], r[0:1, 3, ::-1], row[0:1, 2 + h, ::-1], 0.0, ALU.add, ALU.max))
                    v.tensor_tensor(carry_r[0:1, h, 1:P], r[0:1, 4 + h, 0:P - 1], r[0:1, 0, 1:P], ALU.add)
                    c.link(v.tensor_tensor(carry_r[0:1, 2 + h, 0:P - 1], r[0:1, 6 + h, 1:P], r[0:1, 0, 1:P], ALU.add))
                v.sem_inc(carried, 1)
                v.wait_ge(brought, 64)
                v.tensor_scalar(skip[:, :], key[:, :], edge[:, 0:1], LOW, ALU.not_equal, ALU.mult)
                c.link(v.tensor_scalar(skip_b[:, :], key[:, :], edge[:, 1:2], LOW, ALU.not_equal, ALU.mult))
                for h in range(HEADS):
                    c.link(v.scalar_tensor_tensor(most[:, h, :], skip[:, :], carry[:, h:h + 1], most[:, h, :], ALU.add, ALU.max))
                    c.link(v.scalar_tensor_tensor(most[:, h, :], skip_b[:, :], carry[:, 2 + h:3 + h], most[:, h, :], ALU.add, ALU.max))
                    v.scalar_tensor_tensor(leaky[:, h, :], zk[:, :, h], NEG_SLOPE, zk[:, :, h], ALU.mult, ALU.max)
                    c.link(v.scalar_tensor_tensor(scratch[:, h, :], most[:, h, :], NEG_SLOPE, most[:, h, :], ALU.mult, ALU.max))
                    c.link(v.tensor_tensor(leaky[:, h, :], leaky[:, h, :], scratch[:, h, :], ALU.subtract))
                v.sem_inc(ready, 1)

            @block.scalar
            def _(act):
                act.wait_ge(ready, 1)
                act.activation(scratch[:, :, :], leaky[:, :, :], ACT.Exp).then_inc(raised, 1)


def make_visits(nc, K, T, name, keys, block_row, tile_row, where, others):
    sources = [keys] + [a for a, _ in others]
    targets = [where] + [b for _, b in others]
    with Stage(nc, name) as s:
        last = s.sb("last", [P, GT])
        before = s.sb("before", [P, NB, GT])
        tiles = s.sb("tiles", [P, NB])
        start = s.sb("start", [P, NB])
        begun = s.sb("begun", [P, GV, NB])
        blk = s.sb("blk", [P, GV])
        tile = s.sb("tile", [P, GV])
        blk_i = s.sb("blk_i", [P, GV], I32)
        tile_i = s.sb("tile_i", [P, GV], I32)
        rows = s.sb("rows", [P, 2, P])
        rel = s.sb("rel", [P, 2, P])
        minus = s.sb("minus", [P, GV])
        ps_tiles = s.ps("ps_tiles", [P, 512])
        ps_rows = s.ps("ps_rows", [P, 2, 512])
        loaded, chain, partial, summed, indexed, kept, kept2, shifted, turned, copied = [
            s.sem(n) for n in ("loaded", "chain", "partial", "summed", "indexed", "kept", "kept2", "shifted", "turned", "copied")]
        got = [s.pool_dma_sem(f"got{k}") for k in range(2)]
        jobs = [(j, g) for j in range(len(sources)) for g in range(GV)]
        with nc.Block() as block:
            @block.sync
            def _(sp):
                with nc.allow_non_contiguous_dma(reason="one key of each tile, and tables of a word per visit"):
                    sp.dma_start(last[:, :], keys.rearrange("(g p e) -> p g e", p=P, e=P)[:, :, P - 1:P]).then_inc(loaded, 16)
                    sp.wait_ge(indexed, 1)
                    sp.dma_start(T.blk.rearrange("(g p) -> p g", p=P), blk_i[:, :]).then_inc(kept, 16)
                    sp.dma_start(T.tile.rearrange("(g p) -> p g", p=P), tile_i[:, :]).then_inc(kept, 16)
                sp.wait_ge(kept, 32)
                sp.dma_start(block_row[0:1, :], T.blk.rearrange("(a v) -> a v", a=1)).then_inc(kept2, 16)
                sp.dma_start(tile_row[0:1, :], T.tile.rearrange("(a v) -> a v", a=1)).then_inc(kept2, 16)
                sp.wait_ge(kept2, 32)

            @block.gpsimd
            def _(pool):
                pool.wait_ge(indexed, 1)
                for n, (j, g) in enumerate(jobs):
                    if n >= 2:
                        pool.wait_ge(shifted, n - 1)
                    pool.indirect_dma_start(rows[:, n % 2, :], None, sources[j].rearrange("(t e) -> t e", e=P),
                                            bass.IndirectOffsetOnAxis(tile_i[:, g:g + 1], axis=0)).then_inc(got[n % 2], 16)

            @block.vector
            def _(v):
                c = Chain(v, chain)
                v.wait_ge(loaded, 16)
                for g in range(GT):
                    m = v.tensor_scalar(before[:, :, g], K.edges[:, :], last[:, g:g + 1], None, ALU.is_gt)
                c.link(m)
                v.tensor_reduce(tiles[:, :], before[:, :, :], X_AXIS, ALU.add).then_inc(partial, 1)
                v.wait_ge(summed, 1)
                c.link(v.scalar_tensor_tensor(start[:, :], K.edges[:, :], 1.0 / P, ps_tiles[:, 0:NB], ALU.mult, ALU.add))
                c.link(v.memset(start[:, NB - 1:NB], float(VISITS)))
                for g in range(GV):
                    m = v.tensor_scalar(begun[:, g, :], start[:, :], K.visit[:, g:g + 1], None, ALU.is_le)
                c.link(m)
                c.link(v.tensor_reduce(blk[:, :], begun[:, :, :], X_AXIS, ALU.add))
                c.link(v.tensor_tensor(tile[:, :], K.visit[:, :], blk[:, :], ALU.subtract))
                c.link(v.tensor_scalar(tile[:, :], tile[:, :], float(NT - 1), None, ALU.min))
                v.tensor_copy(blk_i[:, :], blk[:, :])
                v.tensor_scalar(minus[:, :], blk[:, :], -float(P), None, ALU.mult)
                c.link(v.tensor_copy(tile_i[:, :], tile[:, :]))
                v.sem_inc(indexed, 1)
                for n, (j, g) in enumerate(jobs):
                    v.wait_ge(got[n % 2], 16 * (n // 2 + 1))
                    if n >= 2:
                        v.wait_ge(turned, n - 1)
                    if j == 0:
                        v.tensor_scalar(rel[:, n % 2, :], rows[:, n % 2, :], minus[:, g:g + 1], None, ALU.add).then_inc(shifted, 1)
                    else:
                        v.tensor_copy(rel[:, n % 2, :], rows[:, n % 2, :]).then_inc(shifted, 1)

            @block.tensor
            def _(pe):
                pe.wait_ge(partial, 1)
                pe.matmul(ps_tiles[:, 0:NB], K.ones[:, :], tiles[:, :], start=True, stop=True).then_inc(summed, 1)
                for n in range(len(jobs)):
                    pe.wait_ge(shifted, n + 1)
                    if n >= 2:
                        pe.wait_ge(copied, n - 1)
                    pe.transpose(ps_rows[:, n % 2, 0:P], rel[:, n % 2, :], K.ident[:, :]).then_inc(turned, 1)

            @block.scalar
            def _(act):
                for n, (j, g) in enumerate(jobs):
                    act.wait_ge(turned, n + 1)
                    act.copy(targets[j][:, g * P:(g + 1) * P], ps_rows[:, n % 2, 0:P]).then_inc(copied, 1)


REASON = "the table's values are blocks 0 to NB and tiles 0 to NT - 1 by construction"


def sum_attention(nc, K, T, V, total):
    with Stage(nc, "att") as s:
        rows = s.sb("rows", [P, U, ROWP])
        hot = s.sb("hot", [P, U, P])
        scaled = s.sb("scaled", [P, U, HEADS, P])
        ps = s.ps("ps", [P, -(-U // 3), 512])
        built, weighed, multiplied, added = [s.sem(n) for n in ("built", "weighed", "multiplied", "added")]
        got = [s.sem(f"got{k}") for k in range(U)]
        W = HEADS * ROW

        def bank(k):
            return ps[:, k // 3, (k % 3) * W:(k % 3 + 1) * W]

        def bank_end(k):
            return min(k // 3 * 3 + 3, U)

        with nc.Block() as block:
            @block.sync
            def _(sp):
                with sp.Fori(0, NV // U) as i:
                    tiles = load_registers(nc, mybir.EngineType.SP, V.tile_row, i, NT - 1, REASON)
                    for k in range(U):
                        sp.wait_ge(multiplied, i * U + (k + 1))
                        sp.dma_start(rows[:, k, :], T.sorted[bass.ds(tiles[k] * P, P), :]).then_inc(got[k], 16)

            @block.vector
            def _(v):
                def build(i):
                    for k in range(U):
                        v.wait_ge(weighed, i * U + (k + 1))
                        v.tensor_scalar(hot[:, k, :], K.iota[:, :], V.rel[:, at(i * U + k)], None, ALU.is_equal).then_inc(built, 1)

                def add(i):
                    blocks = load_registers(nc, mybir.EngineType.DVE, V.block_row, i, NB, REASON)
                    for k in range(U):
                        v.wait_ge(multiplied, i * U + (U + bank_end(k)))
                        v.wait_ge(added, i * U + (U + k + 1))
                        t = total[:, bass.ds(blocks[k], 1), :, :].rearrange("p o h w -> p (o h w)")
                        v.tensor_tensor(t, t, bank(k), ALU.add).then_inc(added, 1)

                v.sem_inc(added, U)
                v.memset(total[:, :, :, :], 0.0).then_inc(added, 1)
                build(0)
                with v.Fori(1, NV // U) as i:
                    build(i)
                    add(i - 1)
                add(NV // U - 1)

            @block.scalar
            def _(act):
                act.sem_inc(weighed, U)
                with act.Fori(0, NV // U) as i:
                    for k in range(U):
                        act.wait_ge(built, i * U + (k + 1))
                        act.wait_ge(multiplied, i * U + (k + 1))
                        for h in range(HEADS):
                            m = act.activation(scaled[:, k, h, :], hot[:, k, :], ACT.Copy, scale=V.e[h][:, at(i * U + k)])
                        m.then_inc(weighed, 1)

            @block.tensor
            def _(pe):
                pe.sem_inc(multiplied, U)
                with pe.Fori(0, NV // U) as i:
                    for k in range(U):
                        pe.wait_ge(weighed, i * U + (U + k + 1))
                        pe.wait_ge(got[k], i * 16 + 16)
                        pe.wait_ge(added, i * U + (bank_end(k) + 1))
                        for h in range(HEADS):
                            m = pe.matmul(bank(k)[:, h * ROW:(h + 1) * ROW], scaled[:, k, h, :], rows[:, k, 0:ROW], start=True, stop=True)
                        m.then_inc(multiplied, 1)


def finish_attention(nc, K, total):
    with Stage(nc, "proj") as s:
        inv = s.sb("inv", [P, NB, HEADS])
        held = s.sb("held", [P, 2, HEADS, ROW])
        turned = s.sb("turned", [ROW, 2, HEADS, P])
        ps_turn = s.ps("ps_turn", [ROW, 2, 512])
        ps_out = s.ps("ps_out", [P, 2, 512])
        chain, scaled, flipped, copied, projected, added = [
            s.sem(n) for n in ("chain", "scaled", "flipped", "copied", "projected", "added")]
        with nc.Block() as block:
            @block.vector
            def _(v):
                c = Chain(v, chain)
                c.link(v.tensor_scalar(inv[:, :, :], total[:, 0:NB, :, C_ONE], 1e-16, 1.0 / 0.5, ALU.add, ALU.mult))
                c.link(v.reciprocal(inv[:, :, :], inv[:, :, :]))
                c.link(v.tensor_tensor(K.x[:, :, :], K.x[:, :, :], K.bias[:, :].rearrange("p (o d) -> p o d", o=1).to_broadcast([P, NB, D]), ALU.add))
                v.sem_inc(added, 2)
                with v.Fori(0, NB // 2) as i:
                    for k in range(2):
                        v.wait_ge(flipped, i * 2 + (k + 1))
                        for h in range(HEADS):
                            m = v.tensor_scalar(held[:, k, h, :], total[:, bass.ds(i * 2 + k, 1), h, :].rearrange("p o w -> p (o w)"),
                                                inv[:, bass.ds(i * 2 + k, 1), h], None, ALU.mult)
                        m.then_inc(scaled, 1)
                    for k in range(2):
                        v.wait_ge(projected, i * 2 + (k + 3))
                        xb = K.x[:, bass.ds(i * 2 + k, 1), :].rearrange("p o d -> p (o d)")
                        v.tensor_tensor(xb, xb, ps_out[:, k, 0:D], ALU.add).then_inc(added, 1)

            @block.tensor
            def _(pe):
                pe.sem_inc(projected, 2)
                pe.sem_inc(flipped, 2)
                with pe.Fori(0, NB // 2) as i:
                    for k in range(2):
                        pe.wait_ge(copied, i * 2 + (k + 1))
                        pe.wait_ge(scaled, i * 2 + (k + 1))
                        for h in range(HEADS):
                            m = pe.transpose(ps_turn[:, k, h * P:(h + 1) * P], held[:, k, h, :], K.ident[:, :])
                        m.then_inc(flipped, 1)
                    for k in range(2):
                        pe.wait_ge(copied, i * 2 + (k + 3))
                        pe.wait_ge(added, i * 2 + (k + 1))
                        for h in range(HEADS):
                            m = pe.matmul(ps_out[:, k, 0:D], turned[:, k, h, :], K.w_att[:, h * D:(h + 1) * D],
                                          start=(h == 0), stop=(h == HEADS - 1))
                        m.then_inc(projected, 1)

            @block.scalar
            def _(act):
                act.sem_inc(copied, 2)
                with act.Fori(0, NB // 2) as i:
                    for k in range(2):
                        act.wait_ge(flipped, i * 2 + (k + 3))
                        act.wait_ge(projected, i * 2 + (k + 1))
                        act.copy(turned[:, k, :, :].rearrange("w h p -> w (h p)"), ps_turn[:, k, 0:HEADS * P]).then_inc(copied, 1)


def layer_norm(nc, K, name, addend=None):
    with Stage(nc, name) as s:
        sq = s.sb("sq", [P, NB, D])
        mean = s.sb("mean", [P, NB])
        var = s.sb("var", [P, NB])
        chain, ready, rooted = [s.sem(n) for n in ("chain", "ready", "rooted")]

        def wide(a):
            return a[:, :].rearrange("p (b o) -> p b o", o=1).to_broadcast([P, NB, D])

        with nc.Block() as block:
            @block.vector
            def _(v):
                c = Chain(v, chain)
                x = K.x[:, :, :]
                if addend is not None:
                    c.link(v.tensor_tensor(x, x, addend, ALU.add))
                c.link(v.tensor_reduce(mean[:, :], x, X_AXIS, ALU.add))
                c.link(v.tensor_scalar(mean[:, :], mean[:, :], 1.0 / D, None, ALU.mult))
                c.link(v.tensor_tensor(x, x, wide(mean), ALU.subtract))
                c.link(v.tensor_tensor(sq[:, :, :], x, x, ALU.mult))
                c.link(v.tensor_reduce(var[:, :], sq[:, :, :], X_AXIS, ALU.add))
                c.link(v.tensor_scalar(var[:, :], var[:, :], 1.0 / D, EPS, ALU.mult, ALU.add))
                v.sem_inc(ready, 1)
                v.wait_ge(rooted, 1)
                c.link(v.reciprocal(var[:, :], var[:, :]))
                c.link(v.tensor_tensor(x, x, wide(var), ALU.mult))

            @block.scalar
            def _(act):
                act.wait_ge(ready, 1)
                act.activation(var[:, :], var[:, :], ACT.Sqrt).then_inc(rooted, 1)


def relation_table(nc, K, T, w_rel):
    H = RELS * D // 2
    with Stage(nc, "rel") as s:
        w = s.sb("w", [D, RELS, D])
        xt = s.sb("xt", [D, 2, P])
        held = s.sb("held", [P, 2, D])
        y = s.sb("y", [P, 2, 2 * H])
        ps_x = s.ps("ps_x", [D, 2, 512])
        ps_y = s.ps("ps_y", [P, 2, 2, 512])
        loaded, staged, flipped, copied, multiplied, half_a, half_b = [
            s.sem(n) for n in ("loaded", "staged", "flipped", "copied", "multiplied", "half_a", "half_b")]
        stored = [s.sem(f"stored{k}") for k in range(2)]
        passed = s.sem("passed")
        with nc.Block() as block:
            @block.sync
            def _(sp):
                sp.dma_start(w[:, :, :], w_rel.rearrange("r k d -> k r d")).then_inc(loaded, 16)
                for k in range(2):
                    sp.dma_start(T.blank[k:k + 1, :], K.ones[0:1, 0:P]).then_inc(stored[k], 16)
                with sp.Fori(0, NB // 2) as i:
                    for k in range(2):
                        sp.wait_ge(half_a, i * 2 + (k + 3))
                        sp.wait_ge(half_b, i * 2 + (k + 3))
                        sp.dma_start(T.rel[bass.ds((i * 2 + k) * P, P), :], y[:, k, :]).then_inc(stored[k], 16)
                for k in range(2):
                    sp.wait_ge(stored[k], 16 * (NB // 2 + 1))

            @block.gpsimd
            def _(pool):
                with pool.Fori(0, NB // 2) as i:
                    for k in range(2):
                        pool.wait_ge(flipped, i * 2 + (k + 1))
                        pool.tensor_copy(held[:, k, :], K.x[:, bass.ds(i * 2 + k, 1), :].rearrange("p o d -> p (o d)")).then_inc(staged, 1)

            @block.tensor
            def _(pe):
                pe.wait_ge(loaded, 16)
                pe.sem_inc(multiplied, 2)
                pe.sem_inc(flipped, 2)
                with pe.Fori(0, NB // 2) as i:
                    for k in range(2):
                        wait_apart(pe, passed, copied, i * 2 + (k + 1))
                        wait_apart(pe, passed, staged, i * 2 + (k + 1))
                        pe.transpose(ps_x[:, k, 0:P], held[:, k, :], K.ident[:, :]).then_inc(flipped, 1)
                    for k in range(2):
                        pe.wait_ge(copied, i * 2 + (k + 3))
                        pe.wait_ge(half_a, i * 2 + (k + 1))
                        pe.wait_ge(half_b, i * 2 + (k + 1))
                        for half in range(2):
                            m = pe.matmul(ps_y[:, k, half, :], xt[:, k, :], w[:, half * (RELS // 2):(half + 1) * (RELS // 2), :].rearrange("k r d -> k (r d)"),
                                          start=True, stop=True)
                        m.then_inc(multiplied, 1)

            @block.scalar
            def _(act):
                act.sem_inc(copied, 2)
                act.sem_inc(half_a, 2)
                with act.Fori(0, NB // 2) as i:
                    for k in range(2):
                        act.wait_ge(flipped, i * 2 + (k + 3))
                        act.wait_ge(multiplied, i * 2 + (k + 1))
                        act.copy(xt[:, k, :], ps_x[:, k, 0:P]).then_inc(copied, 1)
                    for k in range(2):
                        act.wait_ge(multiplied, i * 2 + (k + 3))
                        act.wait_ge(stored[k], i * 16 + 16)
                        act.copy(y[:, k, 0:H], ps_y[:, k, 0, :]).then_inc(half_a, 1)

            @block.vector
            def _(v):
                v.sem_inc(half_b, 2)
                with v.Fori(0, NB // 2) as i:
                    for k in range(2):
                        v.wait_ge(multiplied, i * 2 + (k + 3))
                        v.wait_ge(stored[k], i * 16 + 16)
                        v.tensor_copy(y[:, k, H:2 * H], ps_y[:, k, 1, :]).then_inc(half_b, 1)


def node_table(nc, K, name, table):
    with Stage(nc, name) as s:
        stored = s.sem("stored")
        with nc.Block() as block:
            @block.sync
            def _(sp):
                sp.dma_start(table.rearrange("(b p) d -> p b d", p=P), K.x[:, :, :]).then_inc(stored, 16)
                sp.wait_ge(stored, 16)


def turn_nodes(nc, K, xt):
    with Stage(nc, "turn") as s:
        ps = s.ps("ps", [D, 2, 512])
        held = s.sb("held", [P, 2, D])
        staged, flipped, copied = s.sem("staged"), s.sem("flipped"), s.sem("copied")
        passed = s.sem("passed")
        with nc.Block() as block:
            @block.gpsimd
            def _(pool):
                with pool.Fori(0, NB // 2) as i:
                    for k in range(2):
                        pool.wait_ge(flipped, i * 2 + (k + 1))
                        pool.tensor_copy(held[:, k, :], K.x[:, bass.ds(i * 2 + k, 1), :].rearrange("p o d -> p (o d)")).then_inc(staged, 1)

            @block.tensor
            def _(pe):
                pe.sem_inc(flipped, 2)
                with pe.Fori(0, NB // 2) as i:
                    for k in range(2):
                        wait_apart(pe, passed, copied, i * 2 + (k + 1))
                        wait_apart(pe, passed, staged, i * 2 + (k + 1))
                        pe.transpose(ps[:, k, 0:P], held[:, k, :], K.ident[:, :]).then_inc(flipped, 1)

            @block.scalar
            def _(act):
                act.sem_inc(copied, 2)
                with act.Fori(0, NB // 2) as i:
                    for k in range(2):
                        act.wait_ge(flipped, i * 2 + (k + 3))
                        act.copy(xt[:, bass.ds((i * 2 + k) * P, P)], ps[:, k, 0:P]).then_inc(copied, 1)

            @block.vector
            def _(v):
                v.memset(xt[:, NP:NP + P], 0.0)


def sum_rows(nc, K, V, name, table, index, total, weight=None, xt=None):
    with Stage(nc, name) as s:
        rows = s.sb("rows", [P, U, D])
        fetch = s.sb("fetch", [P, U], I32)
        hot = s.sb("hot", [P, U, P])
        rows_t = s.sb("rows_t", [D, 2, GROUP * P])
        ps_sum = s.ps("ps_sum", [P, 2, 512])
        ps_turn = s.ps("ps_turn", [D, 2, 512])
        ps_dot = s.ps("ps_dot", [P, 2, 512])
        fetch_ready, built, multiplied, added, turned, copied, dotted, passed = [
            s.sem(n) for n in ("fetch_ready", "built", "multiplied", "added", "turned", "copied", "dotted", "passed")]
        got = [s.pool_dma_sem(f"got{k}") for k in range(U)]
        AHEAD = 2 * GROUP

        def of(g):
            return range(g * GROUP, (g + 1) * GROUP)

        with nc.Block() as block:
            @block.gpsimd
            def _(pool):
                with pool.Fori(0, NV // U) as i:
                    for k in range(U):
                        if k % GROUP == 0:
                            wait_apart(pool, passed, fetch_ready, i * NG + (k // GROUP + 1))
                        wait_apart(pool, passed, multiplied, i * U + (k + 1))
                        pool.indirect_dma_start(rows[:, k, :], None, table,
                                                bass.IndirectOffsetOnAxis(fetch[:, k:k + 1], axis=0)).then_inc(got[k], 16)

            @block.scalar
            def _(act):
                act.sem_inc(copied, 2)
                for g in range(NG):
                    act.copy(fetch[:, g * GROUP:(g + 1) * GROUP], index[:, g * GROUP:(g + 1) * GROUP]).then_inc(fetch_ready, 1)
                with act.Fori(0, NV // U) as i:
                    for g in range(NG):
                        for k in of(g):
                            act.wait_ge(got[k], i * 16 + 16)
                        act.copy(fetch[:, g * GROUP:(g + 1) * GROUP],
                                 index[:, bass.ds(i * U + (U + g * GROUP), GROUP)]).then_inc(fetch_ready, 1)
                        if xt is not None:
                            act.wait_ge(turned, i * NG + (g + 1))
                            act.wait_ge(dotted, i * U + (g + 1) * GROUP)
                            act.copy(rows_t[:, g % 2, :], ps_turn[:, g % 2, :]).then_inc(copied, 1)

            @block.vector
            def _(v):
                v.sem_inc(added, AHEAD)
                v.sem_inc(built, AHEAD)
                v.memset(total[:, :, :], 0.0).then_inc(added, 1)
                with v.Fori(0, NV // U) as i:
                    blocks = load_registers(nc, mybir.EngineType.DVE, V.block_row, i, NB, REASON)
                    for g in range(NG):
                        for k in of(g):
                            v.wait_ge(multiplied, i * U + (k + 1))
                            rel = V.rel[:, at(i * U + k)]
                            if xt is not None:
                                v.wait_ge(dotted, i * U + (AHEAD + (g + 1) * GROUP))
                                m = v.scalar_tensor_tensor(hot[:, k, :], K.iota[:, :], rel,
                                                           ps_dot[:, g % 2, (k % GROUP) * P:(k % GROUP + 1) * P], ALU.is_equal, ALU.mult)
                            elif weight is not None:
                                m = v.tensor_scalar(hot[:, k, :], K.iota[:, :], rel, weight[:, at(i * U + k)], ALU.is_equal, ALU.mult)
                            else:
                                m = v.tensor_scalar(hot[:, k, :], K.iota[:, :], rel, None, ALU.is_equal)
                            m.then_inc(built, 1)
                        for k in of(g):
                            v.wait_ge(multiplied, i * U + (U + (g + 1) * GROUP))
                            v.wait_ge(added, i * U + (AHEAD + k + 1))
                            t = total[:, bass.ds(blocks[k], 1), :].rearrange("p o d -> p (o d)")
                            v.tensor_tensor(t, t, ps_sum[:, g % 2, (k % GROUP) * D:(k % GROUP + 1) * D], ALU.add).then_inc(added, 1)

            @block.tensor
            def _(pe):
                pe.sem_inc(multiplied, U)
                pe.sem_inc(dotted, AHEAD)
                with pe.Fori(0, NV // U) as i:
                    if xt is not None:
                        blocks = load_registers(nc, mybir.EngineType.PE, V.block_row, i, NB, REASON)
                    for g in range(NG):
                        if xt is not None:
                            wait_apart(pe, passed, copied, i * NG + (g + 1))
                            for k in of(g):
                                wait_apart(pe, passed, got[k], i * 16 + 16)
                                m = pe.transpose(ps_turn[:, g % 2, (k % GROUP) * P:(k % GROUP + 1) * P], rows[:, k, :], K.ident[:, :])
                            m.then_inc(turned, 1)
                            pe.wait_ge(copied, i * NG + (g + 3))
                            pe.wait_ge(built, i * U + (g + 1) * GROUP)
                            for k in of(g):
                                pe.matmul(ps_dot[:, g % 2, (k % GROUP) * P:(k % GROUP + 1) * P], rows_t[:, g % 2, (k % GROUP) * P:(k % GROUP + 1) * P],
                                          xt[:, bass.ds(blocks[k] * P, P)], start=True, stop=True).then_inc(dotted, 1)
                        pe.wait_ge(added, i * U + ((g + 1) * GROUP + 1))
                        for k in of(g):
                            pe.wait_ge(got[k], i * 16 + 16)
                            pe.wait_ge(built, i * U + (AHEAD + k + 1))
                            pe.matmul(ps_sum[:, g % 2, (k % GROUP) * D:(k % GROUP + 1) * D], hot[:, k, :], rows[:, k, :],
                                      start=True, stop=True).then_inc(multiplied, 1)


def project_sums(nc, K, total, w_fc):
    with Stage(nc, "fc") as s:
        w = s.sb("w", [D, D])
        turned = s.sb("turned", [D, 2, P])
        ps_w = s.ps("ps_w", [D, 512])
        ps_turn = s.ps("ps_turn", [D, 2, 512])
        ps_out = s.ps("ps_out", [P, 2, 512])
        wt = s.sb("wt", [D, D])
        held = s.sb("held", [P, 2, D])
        loaded, staged, flipped, copied, projected, added = [s.sem(n) for n in ("loaded", "staged", "flipped", "copied", "projected", "added")]
        passed = s.sem("passed")
        with nc.Block() as block:
            @block.sync
            def _(sp):
                sp.dma_start(w[:, :], w_fc).then_inc(loaded, 16)

            @block.gpsimd
            def _(pool):
                with pool.Fori(0, NB // 2) as i:
                    for k in range(2):
                        pool.wait_ge(flipped, i * 2 + (k + 2))
                        pool.tensor_copy(held[:, k, :], total[:, bass.ds(i * 2 + k, 1), :].rearrange("p o d -> p (o d)")).then_inc(staged, 1)

            @block.tensor
            def _(pe):
                pe.sem_inc(projected, 2)
                pe.sem_inc(flipped, 2)
                pe.wait_ge(loaded, 16)
                pe.transpose(ps_w[:, 0:D], w[:, :], K.ident[0:D, 0:D]).then_inc(flipped, 1)
                pe.wait_ge(copied, 3)
                with pe.Fori(0, NB // 2) as i:
                    for k in range(2):
                        wait_apart(pe, passed, copied, i * 2 + (k + 2))
                        wait_apart(pe, passed, staged, i * 2 + (k + 1))
                        pe.transpose(ps_turn[:, k, 0:P], held[:, k, :], K.ident[:, :]).then_inc(flipped, 1)
                    for k in range(2):
                        pe.wait_ge(copied, i * 2 + (k + 4))
                        pe.wait_ge(added, i * 2 + (k + 1))
                        pe.matmul(ps_out[:, k, 0:D], turned[:, k, :], wt[:, :], start=True, stop=True).then_inc(projected, 1)

            @block.scalar
            def _(act):
                act.sem_inc(copied, 2)
                act.wait_ge(flipped, 3)
                act.copy(wt[:, :], ps_w[:, 0:D]).then_inc(copied, 1)
                with act.Fori(0, NB // 2) as i:
                    for k in range(2):
                        act.wait_ge(flipped, i * 2 + (k + 4))
                        act.wait_ge(projected, i * 2 + (k + 1))
                        act.copy(turned[:, k, :], ps_turn[:, k, 0:P]).then_inc(copied, 1)

            @block.vector
            def _(v):
                v.sem_inc(added, 2)
                with v.Fori(0, NB // 2) as i:
                    for k in range(2):
                        v.wait_ge(projected, i * 2 + (k + 3))
                        xb = K.x[:, bass.ds(i * 2 + k, 1), :].rearrange("p o d -> p (o d)")
                        v.tensor_tensor(xb, xb, ps_out[:, k, 0:D], ALU.add).then_inc(added, 1)


def store(nc, K, out):
    with Stage(nc, "store") as s:
        stored = s.sem("stored")
        with nc.Block() as block:
            @block.sync
            def _(sp):
                sp.dma_start(out[0:FULLN * P, :].rearrange("(b p) d -> p b d", p=P), K.x[:, 0:FULLN, :]).then_inc(stored, 16)
                sp.dma_start(out[FULLN * P:N, :], K.x[0:RESTN, FULLN, :]).then_inc(stored, 16)
                sp.wait_ge(stored, 32)

def program(nc, x, src, dst, edge_attr, etype, weight, w_lin, b_lin, w_edge, b_edge, att, bias, w_rel, w_fc, out):

    def dram(name, shape, dt=F32):
        return nc.dram_tensor(name, shape, dt).ap()

    K, T, M = Names(), Names(), Names()
    M.src, M.dst, M.relrow, M.weight = [dram(n, (EP,)) for n in ("m_src", "m_dst", "m_relrow", "m_weight")]
    T.nodes = dram("t_nodes", (NP, D + HEADS))
    T.sorted = dram("t_sorted", (EP, ROWP))
    with ExitStack() as Stage.whole, Stage(nc, "k") as k:
        K.ones, K.iota, K.below, K.above, K.ident = [k.sb(n, [P, P]) for n in ("ones", "iota", "below", "above", "ident")]
        K.iota_b, K.ident_b, K.ident_128 = [k.sb(n, [P, P], BF16) for n in ("iota_b", "ident_b", "ident_128")]
        K.pcol = k.sb("pcol", [P, 1])
        K.visit_i, K.visit = k.sb("visit_i", [P, GV], I32), k.sb("visit", [P, GV])
        K.edges_i, K.edges = k.sb("edges_i", [P, NB], I32), k.sb("edges", [P, NB])
        K.x = k.sb("x", [P, NB, D])
        K.w_att = k.sb("w_att", [ROW, HEADS * D])
        K.bias = k.sb("bias", [P, D])
        K.disorder = k.sb("disorder", [1, 1], I32)
        constants(nc, K)
        with Stage(nc, "a") as a:
            A, G = Names(), Names()
            A.src_i, A.dst_i = a.sb("src_i", [P, NT], I32), a.sb("dst_i", [P, NT + U], I32)
            A.src_f = a.sb("src_f", [P, NT])
            load_edges(nc, K, A, src, dst, etype, weight, x, M)
            G.part = a.sb("part", [P, NT, HEADS])
            G.tail = a.sb("tail", [P, NT, ROW - C_KEY])
            A.s_node = a.sb("s_node", [P, HEADS, NB])
            attention_vectors(nc, K, A, G, w_lin, b_lin, w_edge, b_edge, att, bias, edge_attr, T)
            A.lo_f, A.hi_f = a.sb("lo_f", [P, NT]), a.sb("hi_f", [P, NT])
            A.lo, A.hi = a.sb("lo", [P, NT], BF16), a.sb("hi", [P, NT], BF16)
            A.first = a.sb("first", [P, NB])
            A.key_i = A.src_i
            with Stage(nc, "split") as s:
                split_keys(nc, A, s)
            count_places(nc, K, A, "count")
            sort_attention(nc, K, A, G, T)
        M.records = dram("m_records", (EP, 4))
        order_destinations(nc, K, M)
        M.key, M.e = dram("m_key", (EP,)), [dram(f"m_e{h}", (EP,)) for h in range(HEADS)]
        softmax_weights(nc, K, T, M)
        T.blk, T.tile = dram("t_blk", (NVP,), I32), dram("t_tile", (NVP,), I32)
        T.blank = dram("t_blank", (2, P))
        T.rel = dram("t_rel", (NP, RELS * D))
        with Stage(nc, "v1") as a:
            V = Names()
            V.block_row, V.tile_row = a.sb("block_row", [1, NVP], I32), a.sb("tile_row", [1, NVP], I32)
            V.rel, V.e = a.sb("rel", [P, NVP]), [a.sb(f"e{h}", [P, NVP]) for h in range(HEADS)]
            make_visits(nc, K, T, "mv1", M.key, V.block_row, V.tile_row, V.rel, list(zip(M.e, V.e)))
            total = a.sb("total", [P, NB + 1, HEADS, ROW])
            sum_attention(nc, K, T, V, total)
            finish_attention(nc, K, total)
            layer_norm(nc, K, "ln0")
        with Stage(nc, "v2") as a:
            V = Names()
            V.block_row, V.tile_row = a.sb("block_row", [1, NVP], I32), a.sb("tile_row", [1, NVP], I32)
            V.rel, V.weight, V.src, V.relrow = [a.sb(n, [P, NVP]) for n in ("rel", "weight", "src", "relrow")]
            make_visits(nc, K, T, "mv2", M.dst, V.block_row, V.tile_row, V.rel,
                        [(M.weight, V.weight), (M.src, V.src), (M.relrow, V.relrow)])
            total = a.sb("total", [P, NB + 1, D])
            relation_table(nc, K, T, w_rel)
            sum_rows(nc, K, V, "sum1", T.rel.rearrange("n (r d) -> (n r) d", d=D), V.relrow, total)
            layer_norm(nc, K, "ln1", total[:, 0:NB, :])
            T.x2, T.x3 = dram("t_x2", (NP, D)), dram("t_x3", (NP, D))
            node_table(nc, K, "nt2", T.x2)
            sum_rows(nc, K, V, "sum2", T.x2, V.src, total, weight=V.weight)
            layer_norm(nc, K, "ln2", total[:, 0:NB, :])
            with Stage(nc, "v3") as b:
                xt = b.sb("xt", [D, NP + P])
                node_table(nc, K, "nt3", T.x3)
                turn_nodes(nc, K, xt)
                sum_rows(nc, K, V, "sum3", T.x3, V.src, total, xt=xt)
            project_sums(nc, K, total, w_fc)
            layer_norm(nc, K, "ln3")
        store(nc, K, out)


_INS = ["x", "src", "dst", "edge_attr_5", "edge_type_16", "edge_weight", "L0_gnn_W_lin", "L0_gnn_b_lin", "L0_gnn_W_edge",
        "L0_gnn_b_edge", "L0_gnn_att", "L0_gnn_bias", "L1_gnn_weight", "L3_gnn_fc_weight"]


def kernel(**inputs):
    import numpy as _np
    import concourse.bacc as _bacc
    from concourse import mybir as _mybir
    from concourse.bass_utils import run_bass_kernel_spmd as _run

    nc = _bacc.Bacc("TRN2", target_bir_lowering=False, num_devices=1)
    arrays, args = {}, []
    for name in _INS:
        a = _np.ascontiguousarray(inputs[name])
        arrays[f"in_{name}_dram"] = a
        args.append(nc.dram_tensor(f"in_{name}_dram", a.shape, _mybir.dt.from_np(a.dtype), kind="ExternalInput").ap())
    out = nc.dram_tensor("out_0_dram", (N, D), _mybir.dt.float32, kind="ExternalOutput").ap()
    program(nc, *args, out)
    r = _run(nc, [arrays], core_ids=[0])
    return r.results[0]["out_0_dram"]
```
